# Optimizing a Trainium2 kernel written in Bass

```python
import numpy as np
import jax
import jax.numpy as jnp

def _softmax(x, axis=-1):
    return jax.nn.softmax(x, axis=axis)

def _gelu(x):
    return jax.nn.gelu(x, approximate=True)

def _silu(x):
    return jax.nn.silu(x)

def _sigmoid(x):
    return jax.nn.sigmoid(x)

def _layernorm(x, axis=-1, eps=1e-05):
    m = jnp.mean(x, axis=axis, keepdims=True)
    v = jnp.var(x, axis=axis, keepdims=True)
    return (x - m) / jnp.sqrt(v + eps)

def _scatter_add(tgt, idx, src, axis=0):
    return tgt.at[idx].add(src)

def _segment_sum(src, seg, n):
    return jax.ops.segment_sum(src, seg, n)
kernel_name = 'mk_gnn_resnorm_d2_gnn_r8_94182f'

def setup_inputs(seed: int=0):
    np.random.seed(seed)
    _w = jnp.asarray

    def _rec_inputs():
        import jax
        import jax.numpy as jnp
        _gk = jax.random.key(seed)
        x = -0.0003713 + 1 * jax.random.normal(jax.random.fold_in(_gk, 1), (12500, 128), jnp.float32)
        _s = jax.random.randint(jax.random.fold_in(_gk, 2), (200000,), 0, 12500, jnp.int32)
        _d = jax.random.randint(jax.random.fold_in(_gk, 3), (200000,), 0, 12500, jnp.int32)
        _loop = jnp.arange(12500, dtype=jnp.int32)
        src = jnp.concatenate([_s, _d, _loop])
        dst = jnp.concatenate([_d, _s, _loop])
        _o = jnp.argsort(dst, stable=True)
        src = src[_o]
        dst = dst[_o]
        edge_attr_50 = 0.000154925 + 1.00009 * jax.random.normal(jax.random.fold_in(_gk, 11), (412500, 50), jnp.float32)
        edge_weight = jax.random.uniform(jax.random.fold_in(_gk, 13), (412500,), jnp.float32, 0.0, 0.999998)
        return (x, src, dst, edge_attr_50, edge_weight)
    x, src, dst, edge_attr_50, edge_weight = _rec_inputs()

    def _L0_gnn_setup():
        import jax, jax.numpy as jnp
        import numpy as np
        EPS = 0.0
        key = jax.random.key(seed)
        kx, ke, kw, k1, k2 = jax.random.split(key, 5)
        N, E, D, H = (12500, 75000, 128, 128)
        x = jax.random.normal(kx, (N, D), dtype=jnp.float32)
        edge_index = jax.random.randint(ke, (2, E), 0, N, dtype=jnp.int64)
        edge_weight = jax.random.uniform(kw, (E,), dtype=jnp.float32)
        W1 = jax.random.normal(k1, (D, H), dtype=jnp.float32) * (1.0 / np.sqrt(D))
        b1 = jnp.zeros((H,), dtype=jnp.float32)
        W2 = jax.random.normal(k2, (H, D), dtype=jnp.float32) * (1.0 / np.sqrt(H))
        b2 = jnp.zeros((D,), dtype=jnp.float32)
        return {'x': x, 'edge_index': edge_index, 'edge_weight': edge_weight, 'W1': W1, 'b1': b1, 'W2': W2, 'b2': b2}
    _L0_gnn_all = _L0_gnn_setup()
    _L0_gnn_in = {k: v for k, v in _L0_gnn_all.items() if k in ('W1', 'b1', 'W2', 'b2')}
    del _L0_gnn_all

    def _L1_gnn_setup():
        import jax, jax.numpy as jnp
        import numpy as np
        CUTOFF = 10.0
        LOG2 = float(np.log(2.0))
        N_NODES = 6250
        N_EDGES = 100000
        IN_CH = 128
        FILTERS = 128
        OUT_CH = 128
        N_GAUSS = 50

        def _xavier(key, shape):
            fan_in, fan_out = (shape[1], shape[0])
            bound = float(np.sqrt(6.0 / (fan_in + fan_out)))
            return jax.random.uniform(key, shape, jnp.float32, -bound, bound)
        key = jax.random.key(seed)
        ks = jax.random.split(key, 10)
        h = jax.random.normal(ks[0], (N_NODES, IN_CH), jnp.float32)
        edge_index = jax.random.randint(ks[1], (2, N_EDGES), 0, N_NODES, jnp.int32)
        edge_weight = jax.random.uniform(ks[2], (N_EDGES,), jnp.float32) * CUTOFF
        edge_attr = jax.random.normal(ks[3], (N_EDGES, N_GAUSS), jnp.float32)
        return {'h': h, 'edge_index': edge_index, 'edge_weight': edge_weight, 'edge_attr': edge_attr, 'lin1_w': _xavier(ks[4], (FILTERS, IN_CH)), 'nn_w1': _xavier(ks[5], (FILTERS, N_GAUSS)), 'nn_b1': jnp.zeros((FILTERS,), jnp.float32), 'nn_w2': _xavier(ks[6], (FILTERS, FILTERS)), 'nn_b2': jnp.zeros((FILTERS,), jnp.float32), 'lin2_w': _xavier(ks[7], (OUT_CH, FILTERS)), 'lin2_b': jnp.zeros((OUT_CH,), jnp.float32)}
    _L1_gnn_all = _L1_gnn_setup()
    _L1_gnn_in = {k: v for k, v in _L1_gnn_all.items() if k in ('lin1_w', 'nn_w1', 'nn_b1', 'nn_w2', 'nn_b2', 'lin2_w', 'lin2_b')}
    del _L1_gnn_all
    return {'x': x, 'src': src, 'dst': dst, 'edge_attr_50': edge_attr_50, 'edge_weight': edge_weight, 'L0_gnn_W1': _L0_gnn_in['W1'], 'L0_gnn_b1': _L0_gnn_in['b1'], 'L0_gnn_W2': _L0_gnn_in['W2'], 'L0_gnn_b2': _L0_gnn_in['b2'], 'L1_gnn_lin1_w': _L1_gnn_in['lin1_w'], 'L1_gnn_nn_w1': _L1_gnn_in['nn_w1'], 'L1_gnn_nn_b1': _L1_gnn_in['nn_b1'], 'L1_gnn_nn_w2': _L1_gnn_in['nn_w2'], 'L1_gnn_nn_b2': _L1_gnn_in['nn_b2'], 'L1_gnn_lin2_w': _L1_gnn_in['lin2_w'], 'L1_gnn_lin2_b': _L1_gnn_in['lin2_b']}

def reference(x, src, dst, edge_attr_50, edge_weight, L0_gnn_W1, L0_gnn_b1, L0_gnn_W2, L0_gnn_b2, L1_gnn_lin1_w, L1_gnn_nn_w1, L1_gnn_nn_b1, L1_gnn_nn_w2, L1_gnn_nn_b2, L1_gnn_lin2_w, L1_gnn_lin2_b):
    import jax
    import jax.numpy as jnp

    def _L0_gnn_ref(x, edge_index, edge_weight, W1, b1, W2, b2):
        import jax, jax.numpy as jnp
        import numpy as np
        EPS = 0.0
        N = x.shape[0]
        src, dst = (edge_index[0], edge_index[1])
        msg = edge_weight[:, None] * x[src]
        agg = jax.ops.segment_sum(msg, dst, num_segments=N)
        out = (1.0 + EPS) * x + agg
        h = jax.nn.relu(out @ W1 + b1)
        return h @ W2 + b2

    def _L1_gnn_ref(h, edge_index, edge_weight, edge_attr, lin1_w, nn_w1, nn_b1, nn_w2, nn_b2, lin2_w, lin2_b):
        import jax, jax.numpy as jnp
        import numpy as np
        CUTOFF = 10.0
        LOG2 = float(np.log(2.0))
        N_NODES = 6250
        N_EDGES = 100000
        IN_CH = 128
        FILTERS = 128
        OUT_CH = 128
        N_GAUSS = 50

        def _xavier(key, shape):
            fan_in, fan_out = (shape[1], shape[0])
            bound = float(np.sqrt(6.0 / (fan_in + fan_out)))
            return jax.random.uniform(key, shape, jnp.float32, -bound, bound)
        n_nodes = h.shape[0]
        h1 = h @ lin1_w.T
        c = 0.5 * (jnp.cos(edge_weight * jnp.pi / CUTOFF) + 1.0)
        x = jax.nn.softplus(edge_attr @ nn_w1.T + nn_b1) - LOG2
        W = (jax.nn.softplus(x @ nn_w2.T + nn_b2) - LOG2) * c[:, None]
        msg = W * h1[edge_index[1]]
        agg = jax.ops.segment_sum(msg, edge_index[0], num_segments=n_nodes)
        h2 = h1 + agg
        return h2 @ lin2_w.T + lin2_b
    edge_index = jnp.stack([src, dst])
    x = _layernorm(x + _L0_gnn_ref(x, edge_index, edge_weight, L0_gnn_W1, L0_gnn_b1, L0_gnn_W2, L0_gnn_b2), axis=-1)
    x = _layernorm(x + _L1_gnn_ref(x, edge_index, edge_weight, edge_attr_50, L1_gnn_lin1_w, L1_gnn_nn_w1, L1_gnn_nn_b1, L1_gnn_nn_w2, L1_gnn_nn_b2, L1_gnn_lin2_w, L1_gnn_lin2_b), axis=-1)
    return x

_drawn_inputs = setup_inputs


def setup_inputs(seed=0):
    import zlib

    import numpy as np

    out = dict(_drawn_inputs(seed))
    spreads = {'L0_gnn_b1': (0.0, 0.1),
     'L0_gnn_b2': (0.0, 0.1),
     'L1_gnn_nn_b1': (0.0, 0.1),
     'L1_gnn_nn_b2': (0.0, 0.1),
     'L1_gnn_lin2_b': (0.0, 0.1)}
    factors = {}
    for name, (base, spread) in spreads.items():
        noise = np.random.default_rng([zlib.crc32(name.encode()), seed]).standard_normal(out[name].shape)
        drawn = base * np.exp(spread * noise) if base else spread * noise
        out[name] = jnp.asarray(drawn.astype(out[name].dtype))
    for name, factor in factors.items():
        out[name] = (out[name] * factor).astype(out[name].dtype)
    return out
```

```python
from contextlib import ExitStack

import concourse.bass as bass
from concourse import mybir

D = 128
P = 128
N = 12500
E = 412500
GAUSS = 50
CHUNK = 512
NH = CHUNK // 2
NPAD = -(-N // CHUNK) * CHUNK
SUB = 8
NCH = NPAD // CHUNK
HALF = SUB // 2
HE = HALF * P
TE = SUB * P
T = -(-E // TE)
EPAD = T * TE
NGRP = -(-T // P)
WIN = 64
SPARE = NPAD
TROWS = NPAD + P
NTAB = SUB
MAXJOBS = T * (-(-N // WIN))
LN_EPS = 1e-5
CUTOFF = 10.0
PI = 3.141592653589793


def edge_network_kernel(nc, x_rows, x_cols, src_cols, dst_cols, w_cols, src_rows, dst_rows,
                        attr_cols, W1, b1, W2, b2, lin1T, nn1T, nn2T, nnb2, lin2T, lin2b, out):
    f32, i32, i16, bf16 = mybir.dt.float32, mybir.dt.int32, mybir.dt.int16, mybir.dt.bfloat16
    ALU = mybir.AluOpType
    ACT = mybir.ActivationFunctionType
    AX = mybir.AxisListType
    ds = bass.ds

    ctx = ExitStack()
    with ctx:
        def sb(name, shape, dt):
            return ctx.enter_context(nc.sbuf_tensor(name, shape, dt))

        def sem(name):
            return ctx.enter_context(nc.semaphore(name))

        src16 = nc.dram_tensor("src16", [T, TE], i16, kind="Internal").ap()
        dst16 = nc.dram_tensor("dst16", [T, TE], i16, kind="Internal").ap()
        base_d = nc.dram_tensor("base_d", [NGRP * P, 1], i32, kind="Internal").ap()
        nwin_d = nc.dram_tensor("nwin_d", [NGRP * P, 1], i32, kind="Internal").ap()
        x1_d = nc.dram_tensor("x1_d", [NPAD, D], f32, kind="Internal").ap()
        h1_parts = nc.dram_tensor("h1_parts", [NPAD, 3 * D], bf16, kind="Internal").ap()
        spare = nc.dram_tensor("spare", [32, 16], f32, kind="Internal").ap()
        tabs = [nc.dram_tensor(f"sum_table{k}", [TROWS, D], f32, kind="Internal").ap()
                for k in range(NTAB)]

        srcf = sb("srcf", [P, T * SUB], f32)
        dstf = sb("dstf", [P, T * SUB], f32)
        wgt = sb("wgt", [P, T * SUB], f32)
        scat = sb("scat", [P, T * SUB], i32)
        base = sb("base", [P, T], i32)
        basef = sb("basef", [P, T], f32)
        nwin = sb("nwin", [P, T], i32)
        ident = sb("ident", [P, P], f32)
        tri = sb("tri", [P, P], f32)
        cols = sb("cols", [P, WIN], f32)
        pidx = sb("pidx", [P, 1], f32)
        spare_row = sb("spare_row", [P, 1], f32)
        eps = sb("eps", [P, 1], f32)
        half = sb("half", [P, 1], f32)
        win = sb("win", [P, 1], f32)
        ones3 = sb("ones3", [3, P], bf16)
        bias3 = {n: sb(f"bias3_{n}", [3, HE], bf16) for n in ("b2", "nnb2", "lin2b")}
        zero = sb("zero", [P, 512], f32)
        w_sb = {n: sb(f"w_{n}", [P, D], f32) for n in ("W1", "W2", "lin1T", "nn2T", "lin2T")}
        nn1 = sb("nn1", [GAUSS + 1, D], f32)
        b1c = sb("b1c", [P, 1], f32)
        bank = [ctx.enter_context(nc.psum_tensor(f"bank{i}", [P, 512], f32)) for i in range(8)]

        with ExitStack() as c0:
            def sb0(name, shape, dt):
                return c0.enter_context(nc.sbuf_tensor(name, shape, dt))

            rows_i = sb0("rows_i", [P, NGRP, 2, TE], i32)
            rows_h = sb0("rows_h", [P, NGRP, 2, TE], i16)
            cols_i = sb0("cols_i", [P, 2, T * SUB], i32)
            least = sb0("least", [P, NGRP], i32)
            most = sb0("most", [P, NGRP], i32)
            brow = sb0("brow", [1, 3, D], f32)
            bpart = sb0("bpart", [1, 3, 3, 4, D], bf16)
            brest = sb0("brest", [1, 2, 3, D], f32)
            s_rows, s_cols, s_w = sem("rows_loaded"), sem("cols_loaded"), sem("weights_loaded")
            s_brow, s_const, s_pool = sem("bias_rows"), sem("consts"), sem("pool_consts")
            s_win, s_half, s_split = sem("windows"), sem("halved"), sem("split_step")
            s_st, s_tab, s_b3, s_zero = sem("scratch_stored"), sem("table_loaded"), sem("bias_moved"), sem("zeroed")
            s_fin, s_dv = sem("setup_cols"), sem("window_steps")
            g = [min(P, T - P * i) for i in range(NGRP)]

            with nc.Block() as block:
                @block.sync
                def _(sp):
                    for i in range(NGRP):
                        sp.dma_start(rows_i[0:g[i], i, 0, :], dst_rows[P * i:P * i + g[i], :]).then_inc(s_rows, 16)
                        sp.dma_start(rows_i[0:g[i], i, 1, :], src_rows[P * i:P * i + g[i], :]).then_inc(s_rows, 16)
                    for n, v in (("W1", W1), ("W2", W2), ("lin1T", lin1T), ("nn2T", nn2T), ("lin2T", lin2T)):
                        sp.dma_start(w_sb[n][:, :], v).then_inc(s_w, 16)
                    sp.dma_start(nn1[:, :], nn1T).then_inc(s_w, 16)
                    sp.dma_start(b1c[:, :], b1).then_inc(s_w, 16)
                    sp.wait_ge(s_split, 5)
                    for i, n in enumerate(("b2", "nnb2", "lin2b")):
                        for k in range(3):
                            sp.dma_start(bias3[n][k:k + 1, :], bpart[0:1, k, i, :, :].rearrange("o a d -> o (a d)")).then_inc(s_b3, 16)
                    sp.wait_ge(s_win, 1)
                    for i in range(NGRP):
                        sp.dma_start(base_d[P * i:P * i + g[i], :], least[0:g[i], i:i + 1]).then_inc(s_st, 16)
                        sp.dma_start(nwin_d[P * i:P * i + g[i], :], most[0:g[i], i:i + 1]).then_inc(s_st, 16)
                    sp.wait_ge(s_half, NGRP)
                    for i in range(NGRP):
                        sp.dma_start(dst16[P * i:P * i + g[i], :], rows_h[0:g[i], i, 0, :]).then_inc(s_st, 16)
                        sp.dma_start(src16[P * i:P * i + g[i], :], rows_h[0:g[i], i, 1, :]).then_inc(s_st, 16)
                    sp.wait_ge(s_st, 16 * 4 * NGRP)
                    sp.dma_start(base[:, :], base_d[0:T, :].rearrange("t o -> o t").broadcast_to([P, T])).then_inc(s_tab, 16)
                    sp.dma_start(nwin[:, :], nwin_d[0:T, :].rearrange("t o -> o t").broadcast_to([P, T])).then_inc(s_tab, 16)
                    sp.wait_ge(s_w, 16 * 7)
                    sp.wait_ge(s_b3, 16 * 9)
                    sp.wait_ge(s_tab, 32)

                @block.scalar
                def _(act):
                    act.dma_start(cols_i[:, 0, :], src_cols).then_inc(s_cols, 16)
                    act.dma_start(cols_i[:, 1, :], dst_cols).then_inc(s_cols, 16)
                    act.dma_start(wgt[:, :], w_cols).then_inc(s_cols, 16)
                    for i, v in enumerate((b2, nnb2, lin2b)):
                        act.dma_start(brow[0:1, i, :], v).then_inc(s_brow, 16)
                    act.wait_ge(s_cols, 48)
                    nc.scalar.activation(srcf[:, :], cols_i[:, 0, :], ACT.Copy).then_inc(s_fin, 1)
                    nc.scalar.activation(dstf[:, :], cols_i[:, 1, :], ACT.Copy).then_inc(s_fin, 1)

                @block.gpsimd
                def _(pool):
                    pool.memset(zero[:, :], 0.0).then_inc(s_zero, 1)
                    pool.memset(ident[:, :], 0.0).then_inc(s_pool, 1)
                    pool.memset(tri[:, :], 1.0).then_inc(s_pool, 1)
                    pool.memset(ones3[:, :], 1.0).then_inc(s_pool, 1)
                    pool.memset(half[:, :], 0.5).then_inc(s_pool, 1)
                    pool.memset(eps[:, :], LN_EPS).then_inc(s_pool, 1)
                    pool.iota(cols[:, :], pattern=[[1, WIN]], base=0, channel_multiplier=0,
                              allow_small_or_imprecise_dtypes=True).then_inc(s_pool, 1)
                    pool.iota(pidx[:, :], pattern=[[0, 1]], base=0, channel_multiplier=1,
                              allow_small_or_imprecise_dtypes=True).then_inc(s_pool, 1)
                    pool.iota(spare_row[:, :], pattern=[[0, 1]], base=SPARE, channel_multiplier=1,
                              allow_small_or_imprecise_dtypes=True).then_inc(s_pool, 1)
                    pool.wait_ge(s_pool, 8)
                    pool.affine_select(out=ident[:, :], in_=ident[:, :], compare_op=ALU.not_equal, fill=1.0,
                                       base=0, pattern=[[-1, P]], channel_multiplier=1)
                    pool.affine_select(out=tri[:, :], in_=tri[:, :], compare_op=ALU.is_gt, fill=0.0,
                                       base=0, pattern=[[-1, P]], channel_multiplier=1)
                    pool.wait_ge(s_zero, 1)
                    for k in range(NTAB):
                        if k:
                            pool.dma_start(tabs[k][0:NPAD, :].rearrange("(p a) d -> p (a d)", p=P)
                                           .rearrange("p (r c) -> p r c", c=512),
                                           zero[:, :].rearrange("p (o c) -> p o c", o=1)
                                           .broadcast_to([P, NPAD * D // P // 512, 512])).then_inc(s_const, 16)
                        pool.dma_start(tabs[k][NPAD:TROWS, :], zero[:, 0:D]).then_inc(s_const, 16)
                    pool.wait_ge(s_const, 16 * (2 * NTAB - 1))

                @block.vector
                def _(dve):
                    dve.wait_ge(s_rows, 32 * NGRP)
                    for i in range(NGRP):
                        dve.tensor_copy(rows_h[0:g[i], i, :, :], rows_i[0:g[i], i, :, :]).then_inc(s_half, 1)
                    for i in range(NGRP):
                        dve.tensor_reduce(least[0:g[i], i:i + 1], rows_i[0:g[i], i, 0, :], axis=AX.X, op=ALU.min).then_inc(s_dv, 1)
                        dve.tensor_reduce(most[0:g[i], i:i + 1], rows_i[0:g[i], i, 0, :], axis=AX.X, op=ALU.max).then_inc(s_dv, 1)
                    at = 2 * NGRP
                    for op in (lambda a, b: dve.tensor_tensor(a, a, b, ALU.subtract),
                               lambda a, b: dve.tensor_single_scalar(a, a, 6, ALU.arith_shift_right),
                               lambda a, b: dve.tensor_single_scalar(a, a, 1, ALU.add)):
                        dve.wait_ge(s_dv, at)
                        for i in range(NGRP):
                            op(most[0:g[i], i:i + 1], least[0:g[i], i:i + 1]).then_inc(s_dv, 1)
                        at += NGRP
                    dve.wait_ge(s_dv, at)
                    dve.sem_inc(s_win, 1)
                    dve.wait_ge(s_brow, 48)
                    hi, mid, lo = (bpart[0:1, k, :, 0, :] for k in range(3))
                    dve.tensor_copy(hi, brow[:, :, :]).then_inc(s_split, 1)
                    dve.wait_ge(s_split, 1)
                    dve.tensor_tensor(brest[:, 0, :, :], brow[:, :, :], hi, ALU.subtract).then_inc(s_split, 1)
                    dve.wait_ge(s_split, 2)
                    dve.tensor_copy(mid, brest[:, 0, :, :]).then_inc(s_split, 1)
                    dve.wait_ge(s_split, 3)
                    dve.tensor_tensor(lo, brest[:, 0, :, :], mid, ALU.subtract).then_inc(s_split, 1)
                    dve.wait_ge(s_split, 4)
                    dve.tensor_copy(bpart[:, :, :, 1:4, :].rearrange("o k i a d -> o (k i) a d"),
                                    bpart[:, :, :, 0:1, :].rearrange("o k i a d -> o (k i) a d")
                                    .broadcast_to([1, 9, 3, D])).then_inc(s_split, 1)
                    dve.wait_ge(s_tab, 32)
                    dve.tensor_copy(basef[:, :], base[:, :])

        with ExitStack() as c1:
            def sb1(name, shape, dt):
                return c1.enter_context(nc.sbuf_tensor(name, shape, dt))

            aggT = sb1("aggT", [D, NPAD], f32)
            with ExitStack() as c2:
                def sb2(name, shape, dt):
                    return c2.enter_context(nc.sbuf_tensor(name, shape, dt))

                gidx = [sb2(f"gidx{h}", [P, HALF], i32) for h in range(2)]
                xg = [sb2(f"xg{s}", [P, D], f32) for s in range(SUB)]
                onehot = [sb2(f"onehot{s}", [P, WIN], f32) for s in range(SUB)]
                srcb = [sb2(f"srcb{h}", [P, HE], i16) for h in range(2)]
                eq = sb2("eq", [P, P], f32)
                dup = sb2("dup", [P, SUB], f32)
                rel = sb2("rel", [P, SUB], f32)
                mv1 = sb2("mv1", [P, SUB], f32)
                mv2 = sb2("mv2", [P, SUB], f32)
                x_loaded = sem("x_loaded")
                gidx_ready = [sem(f"gidx_ready{h}") for h in range(2)]
                gathered = [sem(f"gathered{s}") for s in range(SUB)]
                summed = sem("summed")
                onehot_ready = sem("onehot_ready")
                srcb_ready = [sem(f"srcb_ready{h}") for h in range(2)]
                dups_done = sem("dups_done")
                flushed = sem("flushed")
                tile_set, win_set, rel_set = sem("tile_set"), sem("win_set"), sem("rel_set")
                passed, passed_dve = sem("passed_pool"), sem("passed_dve")
                mv_set, scat_set, dup_set, eq_used = sem("mv_set"), sem("scat_set"), sem("dup_set"), sem("eq_used")

                with nc.Block() as block:
                    @block.sync
                    def _(sp):
                        sp.dma_start(aggT[:, :], x_cols).then_inc(x_loaded, 16)
                        job = sp.alloc_register("sp_job0")
                        sp.reg_mov(job, 0)
                        with sp.Fori(0, T) as t:
                            windows = sp.value_load(nwin[0:1, ds(t, 1)], min_val=1, max_val=-(-N // WIN))
                            with sp.Fori(0, windows):
                                j = sp.snap(job, min_val=0, max_val=MAXJOBS)
                                for h in range(2):
                                    sp.wait_ge(dups_done, 2 * j + h + 1)
                                    sp.dma_start(srcb[h][:, :], src16[ds(t, 1), h * HE:(h + 1) * HE]
                                                 .broadcast_to([P, HE])).then_inc(srcb_ready[h], 16)
                                sp.reg_add(job, job, 1)
                        sp.wait_ge(x_loaded, 16)

                    @block.scalar
                    def _(act):
                        job = act.alloc_register("act_job0")
                        act.reg_mov(job, 0)
                        with act.Fori(0, T) as t:
                            windows = act.value_load(nwin[0:1, ds(t, 1)], min_val=1, max_val=-(-N // WIN))
                            with act.Fori(0, windows):
                                j = act.snap(job, min_val=0, max_val=MAXJOBS)
                                for h in range(2):
                                    for s in range(HALF * h, HALF * h + HALF):
                                        act.wait_ge(gathered[s], 16 * (j + 1))
                                    nc.scalar.activation(gidx[h][:, :], srcf[:, ds(t * SUB + HALF * h, HALF)],
                                                         ACT.Copy).then_inc(gidx_ready[h], 1)
                                act.reg_add(job, job, 1)

                    @block.gpsimd
                    def _(pool):
                        for s in range(SUB):
                            prime(pool, spare[s:s + 1, :], gathered[s], zero)
                        job = pool.alloc_register("pool_job0")
                        pool.reg_mov(job, 0)
                        with pool.Fori(0, T) as t:
                            windows = pool.value_load(nwin[0:1, ds(t, 1)], min_val=1, max_val=-(-N // WIN))
                            with pool.Fori(0, windows):
                                j = pool.snap(job, min_val=0, max_val=MAXJOBS)
                                for s in range(SUB):
                                    if s % HALF == 0:
                                        pool.wait_ge(gidx_ready[s // HALF], j + 1)
                                    wait_apart(pool, summed, SUB * j + s + 1, passed)
                                    pool.indirect_dma_start(
                                        xg[s][:, :], None, x_rows,
                                        bass.IndirectOffsetOnAxis(ap=gidx[s // HALF][:, s % HALF:s % HALF + 1], axis=0),
                                    ).then_inc(gathered[s], 16)
                                pool.reg_add(job, job, 1)

                    @block.tensor
                    def _(pe):
                        pe.sem_inc(summed, SUB)
                        job = pe.alloc_register("pe_job0")
                        pe.reg_mov(job, 0)
                        with pe.Fori(0, T) as t:
                            windows = pe.value_load(nwin[0:1, ds(t, 1)], min_val=1, max_val=-(-N // WIN))
                            with pe.Fori(0, windows):
                                j = pe.snap(job, min_val=0, max_val=MAXJOBS)
                                for s in range(SUB):
                                    h = s // HALF
                                    if s % HALF == 0:
                                        pe.wait_ge(flushed, 2 * j + h + 1)
                                    pe.wait_ge(gathered[s], 16 * (j + 2))
                                    pe.wait_ge(onehot_ready, SUB * j + s + 1)
                                    nc.tensor.matmul(bank[h][:, 0:WIN], xg[s][:, :], onehot[s][:, :],
                                                     start=(s % HALF == 0), stop=(s % HALF == HALF - 1)).then_inc(summed, 1)
                                pe.reg_add(job, job, 1)

                    @block.vector
                    def _(dve):
                        dve.sem_inc(dups_done, 2)
                        dve.sem_inc(flushed, 2)
                        dve.sem_inc(rel_set, 1)
                        dve.sem_inc(dup_set, 1)
                        dve.wait_ge(x_loaded, 16)
                        job, first = dve.alloc_register("dve_job0"), dve.alloc_register("dve_first0")
                        dve.reg_mov(job, 0)
                        with dve.Fori(0, T) as t:
                            windows = dve.value_load(nwin[0:1, ds(t, 1)], min_val=1, max_val=-(-N // WIN))
                            dve.reg_mov(first, dve.value_load(base[0:1, ds(t, 1)], min_val=0, max_val=NPAD - WIN))
                            here = t * SUB
                            dve.tensor_single_scalar(win[:, :], basef[:, ds(t, 1)], float(WIN), ALU.subtract).then_inc(tile_set, 1)
                            wait_apart(dve, tile_set, t + 1, passed_dve)
                            with dve.Fori(0, windows):
                                j = dve.snap(job, min_val=0, max_val=MAXJOBS)
                                node = dve.snap(first, min_val=0, max_val=NPAD - WIN)
                                dve.wait_ge(rel_set, j + 1)
                                dve.tensor_single_scalar(win[:, :], win[:, :], float(WIN), ALU.add).then_inc(win_set, 1)
                                dve.wait_ge(win_set, j + 1)
                                dve.tensor_single_scalar(rel[:, :], dstf[:, ds(here, SUB)], win[:, 0:1], ALU.subtract).then_inc(rel_set, 1)
                                dve.wait_ge(rel_set, j + 2)
                                for s in range(SUB):
                                    dve.wait_ge(summed, SUB * j + s + 1)
                                    dve.tensor_scalar(onehot[s][:, :], cols[:, :], rel[:, s:s + 1], wgt[:, ds(here + s, 1)],
                                                      ALU.is_equal, ALU.mult).then_inc(onehot_ready, 1)
                                for s in range(SUB):
                                    h, o = s // HALF, (s % HALF) * P
                                    if s % HALF == 0:
                                        dve.wait_ge(srcb_ready[h], 16 * (j + 1))
                                    dve.wait_ge(dup_set, SUB * j + s + 1)
                                    ins = dve.scalar_tensor_tensor(eq[:, :], srcb[h][:, o:o + P], srcf[:, ds(here + s, 1)], tri[:, :],
                                                                   ALU.is_equal, ALU.mult, accum_out=dup[:, s:s + 1])
                                    ins.then_inc(dup_set, 1)
                                    if s % HALF == HALF - 1:
                                        dve.wait_ge(dup_set, SUB * j + s + 2)
                                        dve.sem_inc(dups_done, 1)
                                dve.tensor_scalar(mv1[:, :], srcf[:, ds(here, SUB)], spare_row[:, 0:1], -1.0,
                                                  ALU.subtract, ALU.mult).then_inc(mv_set, 1)
                                dve.wait_ge(mv_set, 2 * j + 1)
                                dve.scalar_tensor_tensor(mv2[:, :], dup[:, :], 1.0, mv1[:, :], ALU.min, ALU.mult).then_inc(mv_set, 1)
                                dve.wait_ge(mv_set, 2 * j + 2)
                                dve.tensor_tensor(scat[:, ds(here, SUB)], mv2[:, :], srcf[:, ds(here, SUB)], ALU.add).then_inc(scat_set, 1)
                                dve.wait_ge(scat_set, j + 1)
                                for h in range(2):
                                    dve.wait_ge(summed, SUB * (j + 1) + HALF * (h + 1))
                                    dve.wait_ge(flushed, 2 * j + 2 + h)
                                    dve.tensor_tensor(aggT[:, ds(node, WIN)], aggT[:, ds(node, WIN)], bank[h][:, 0:WIN],
                                                      ALU.add).then_inc(flushed, 1)
                                dve.reg_add(job, job, 1)
                                dve.reg_add(first, first, WIN)

            layer0_nodes(nc, sem, sb1, aggT, x_rows, x1_d, h1_parts, tabs[0], w_sb, b1c, bias3, ones3, ident, eps, zero, spare, bank)

        with ExitStack() as c3:
            layer1_cutoff(nc, sem, lambda n, s, d: c3.enter_context(nc.sbuf_tensor(n, s, d)), wgt)
        with ExitStack() as c4:
            layer1_edges(nc, sem, lambda n, s, d: c4.enter_context(nc.sbuf_tensor(n, s, d)), src16, dst16, attr_cols,
                         h1_parts, tabs, srcf, wgt, scat, basef, base, nwin, pidx, half, ones3, zero, spare, bias3, nn1, w_sb["nn2T"], bank)
        with ExitStack() as c5:
            layer1_nodes(nc, sem, lambda n, s, d: c5.enter_context(nc.sbuf_tensor(n, s, d)), x1_d, tabs, w_sb["lin2T"],
                         bias3, ones3, ident, eps, zero, spare, bank, out)


def done(c, h):
    return 2 * c + h + 3


def freed(c, h):
    return 2 * c + h + 1


def prime(engine, spare, semaphore, zero):
    engine.dma_start(spare, zero[0:1, 0:16]).then_inc(semaphore, 16)


def wait_apart(engine, semaphore, value, passed):
    engine.wait_ge(semaphore, value)
    engine.sem_inc(passed, 1)


LN_STEPS = 16


def layer_norm_stats(dve, steps, passed, at, y, stats, mean_var):
    wait_apart(dve, steps, at + 1, passed)
    for i in range(2):
        dve.bn_stats(stats[:, i, :], y[:, i, :]).then_inc(steps, 1)
    wait_apart(dve, steps, at + 3, passed)
    for i in range(2):
        dve.bn_aggr(mean_var[:, i, :], stats[:, i, :]).then_inc(steps, 1)


def layer_norm_apply(dve, steps, passed, at, y, mean_var, std, rstd, rows):
    ALU = mybir.AluOpType
    dve.reciprocal(rstd[:, :], std[:, :]).then_inc(steps, 1)
    wait_apart(dve, steps, at + 1, passed)
    for i in range(2):
        dve.tensor_scalar(rows[:, i, :], y[:, i, :], mean_var[:, i, 0:1], rstd[:, i:i + 1],
                          ALU.subtract, ALU.mult).then_inc(steps, 1)


def layer0_nodes(nc, sem, sbuf, aggT, x_rows, x1_d, h1_parts, tab0, w_sb, b1c, bias3, ones3, ident, eps, zero, spare, bank):
    f32, bf16 = mybir.dt.float32, mybir.dt.bfloat16
    ALU, ACT, ds = mybir.AluOpType, mybir.ActivationFunctionType, bass.ds
    hidT = [sbuf(f"n_hidT{h}", [P, NH], f32) for h in range(2)]
    xr = [sbuf(f"n_xr{h}", [P, 2, D], f32) for h in range(2)]
    y = [sbuf(f"n_y{h}", [P, 2, D], f32) for h in range(2)]
    x1 = [sbuf(f"n_x1{h}", [P, 2, D], f32) for h in range(2)]
    x1T = [sbuf(f"n_x1T{h}", [P, NH], f32) for h in range(2)]
    h1 = [sbuf(f"n_h1{h}", [P, 2, D], f32) for h in range(2)]
    parts = [sbuf(f"n_parts{h}", [P, 2, 3, D], bf16) for h in range(2)]
    rest = [sbuf(f"n_rest{h}", [P, 2, 2, D], f32) for h in range(2)]
    stats = [sbuf(f"n_stats{h}", [P, 2, 6], f32) for h in range(2)]
    mean_var = [sbuf(f"n_mv{h}", [P, 2, 2], f32) for h in range(2)]
    std = [sbuf(f"n_std{h}", [P, 2], f32) for h in range(2)]
    rstd = [sbuf(f"n_rstd{h}", [P, 2], f32) for h in range(2)]
    var_set, std_set, passed = sem("n_var_set"), sem("n_std_set"), sem("n_passed")
    up, hid, down, turned, turned_out, lin = (sem(f"n_{n}") for n in ("up", "hid", "down", "turned", "turned_out", "lin"))
    x1_set, h1_set, parts_set, steps = sem("n_x1_set"), sem("n_h1_set"), sem("n_parts_set"), sem("n_steps")
    split = sem("n_split")
    xr_ready = [sem(f"n_xr_ready{h}") for h in range(2)]
    x1_stored, h1_stored, parts_stored = ([sem(f"n_{n}_stored{h}") for h in range(2)] for n in ("x1", "h1", "parts"))

    with nc.Block() as block:
        @block.sync
        def _(sp):
            for h in range(2):
                for k, stored in enumerate((x1_stored, h1_stored, parts_stored)):
                    prime(sp, spare[8 + 3 * h + k:9 + 3 * h + k, :], stored[h], zero)
            with sp.Fori(0, NCH) as c:
                for h in range(2):
                    sp.wait_ge(x1_set, freed(c, h))
                    sp.dma_start(xr[h][:, :, :], x_rows[ds(c * CHUNK + h * NH, NH), :].rearrange("(i p) d -> p i d", p=P)).then_inc(xr_ready[h], 16)
                for h in range(2):
                    sp.wait_ge(x1_set, done(c, h))
                    sp.dma_start(x1_d[ds(c * CHUNK + h * NH, NH), :].rearrange("(i p) d -> p i d", p=P), x1[h][:, :, :]).then_inc(x1_stored[h], 16)
                for h in range(2):
                    sp.wait_ge(h1_set, done(c, h))
                    sp.dma_start(tab0[ds(c * CHUNK + h * NH, NH), :].rearrange("(i p) d -> p i d", p=P), h1[h][:, :, :]).then_inc(h1_stored[h], 16)
                    sp.wait_ge(parts_set, done(c, h))
                    sp.dma_start(h1_parts[ds(c * CHUNK + h * NH, NH), :].rearrange("(i p) d -> p i d", p=P),
                                 parts[h][:, :, :, :].rearrange("p i k d -> p i (k d)")).then_inc(parts_stored[h], 16)
            for h in range(2):
                sp.wait_ge(x1_stored[h], 16 * (NCH + 1))
                sp.wait_ge(h1_stored[h], 16 * (NCH + 1))
                sp.wait_ge(parts_stored[h], 16 * (NCH + 1))

        @block.tensor
        def _(pe):
            for s in (up, down, turned, lin):
                pe.sem_inc(s, 2)
            with pe.Fori(0, NCH) as c:
                for h in range(2):
                    pe.wait_ge(hid, freed(c, h))
                    nc.tensor.matmul(bank[h][:, 0:NH], w_sb["W1"][:, :], aggT[:, ds(c * CHUNK + h * NH, NH)],
                                     start=True, stop=True).then_inc(up, 1)
                for h in range(2):
                    pe.wait_ge(hid, done(c, h))
                    pe.wait_ge(x1_set, freed(c, h))
                    nc.tensor.matmul(bank[2 + h][:, 0:NH], ones3[:, :], bias3["b2"][:, 0:NH], start=True, stop=False)
                    for i in range(2):
                        ins = nc.tensor.matmul(bank[2 + h][:, i * P:i * P + P], hidT[h][:, i * P:i * P + P], w_sb["W2"][:, :],
                                               start=False, stop=(i == 1))
                    ins.then_inc(down, 1)
                for h in range(2):
                    pe.wait_ge(x1_set, done(c, h))
                    pe.wait_ge(turned_out, freed(c, h))
                    for i in range(2):
                        ins = nc.tensor.transpose(bank[4 + h][:, i * P:i * P + P], x1[h][:, i, :], ident[:, :])
                    ins.then_inc(turned, 1)
                for h in range(2):
                    pe.wait_ge(turned_out, done(c, h))
                    pe.wait_ge(h1_set, freed(c, h))
                    for i in range(2):
                        ins = nc.tensor.matmul(bank[6 + h][:, i * P:i * P + P], x1T[h][:, i * P:i * P + P], w_sb["lin1T"][:, :],
                                               start=True, stop=True)
                    ins.then_inc(lin, 1)

        @block.scalar
        def _(act):
            for s in (hid, turned_out, h1_set, std_set):
                act.sem_inc(s, 2)
            with act.Fori(0, NCH) as c:
                for h in range(2):
                    act.wait_ge(up, done(c, h))
                    act.wait_ge(down, freed(c, h))
                    nc.scalar.activation(hidT[h][:, :], bank[h][:, 0:NH], ACT.Relu, bias=b1c[:, 0:1]).then_inc(hid, 1)
                for h in range(2):
                    act.wait_ge(var_set, done(c, h))
                    nc.scalar.activation(std[h][:, :], mean_var[h][:, :, 1], ACT.Sqrt, bias=eps[:, 0:1]).then_inc(std_set, 1)
                for h in range(2):
                    act.wait_ge(turned, done(c, h))
                    act.wait_ge(lin, freed(c, h))
                    nc.scalar.activation(x1T[h][:, :], bank[4 + h][:, 0:NH], ACT.Copy).then_inc(turned_out, 1)
                for h in range(2):
                    act.wait_ge(lin, done(c, h))
                    act.wait_ge(h1_stored[h], 16 * (c + 1))
                    act.wait_ge(parts_set, freed(c, h))
                    nc.scalar.activation(h1[h][:, :, :], bank[6 + h][:, 0:NH].rearrange("p (i d) -> p i d", i=2),
                                         ACT.Copy).then_inc(h1_set, 1)

        @block.vector
        def _(dve):
            for s in (x1_set, parts_set, var_set):
                dve.sem_inc(s, 2)
            with dve.Fori(0, NCH) as c:
                for h in range(2):
                    dve.wait_ge(down, done(c, h))
                    dve.wait_ge(xr_ready[h], 16 * (c + 1))
                    dve.wait_ge(x1_stored[h], 16 * (c + 1))
                    dve.wait_ge(turned, freed(c, h))
                    dve.tensor_tensor(y[h][:, :, :], bank[2 + h][:, 0:NH].rearrange("p (i d) -> p i d", i=2),
                                      xr[h][:, :, :], ALU.add).then_inc(steps, 1)
                    layer_norm_stats(dve, steps, passed, LN_STEPS * c + 5 * h, y[h], stats[h], mean_var[h])
                    dve.wait_ge(steps, LN_STEPS * c + 5 * h + 5)
                    dve.sem_inc(var_set, 1)
                for h in range(2):
                    dve.wait_ge(std_set, done(c, h))
                    layer_norm_apply(dve, steps, passed, LN_STEPS * c + 10 + 3 * h, y[h], mean_var[h], std[h], rstd[h], x1[h])
                    dve.wait_ge(steps, LN_STEPS * c + 13 + 3 * h)
                    dve.sem_inc(x1_set, 1)
                for h in range(2):
                    b = h1[h][:, :, :]
                    at = 8 * c + 4 * h
                    dve.wait_ge(h1_set, done(c, h))
                    dve.wait_ge(parts_stored[h], 16 * (c + 1))
                    dve.tensor_copy(parts[h][:, :, 0, :], b).then_inc(split, 1)
                    dve.wait_ge(split, at + 1)
                    dve.tensor_tensor(rest[h][:, :, 0, :], b, parts[h][:, :, 0, :], ALU.subtract).then_inc(split, 1)
                    dve.wait_ge(split, at + 2)
                    dve.tensor_copy(parts[h][:, :, 1, :], rest[h][:, :, 0, :]).then_inc(split, 1)
                    dve.wait_ge(split, at + 3)
                    dve.tensor_tensor(parts[h][:, :, 2, :], rest[h][:, :, 0, :], parts[h][:, :, 1, :], ALU.subtract).then_inc(split, 1)
                    dve.wait_ge(split, at + 4)
                    dve.sem_inc(parts_set, 1)


def layer1_cutoff(nc, sem, sbuf, wgt):
    ALU, ACT = mybir.AluOpType, mybir.ActivationFunctionType
    f32 = mybir.dt.float32
    turns = sbuf("turns", [P, T * SUB], f32)
    u = sbuf("u", [P, T * SUB], f32)
    half_pi = sbuf("half_pi", [P, 1], f32)
    steps, sined = sem("c_steps"), sem("c_sined")
    magic = 1.5 * 2.0 ** 23

    with nc.Block() as block:
        @block.vector
        def _(dve):
            dve.memset(half_pi[:, :], PI / 2).then_inc(steps, 1)
            dve.tensor_scalar(turns[:, :], wgt[:, :], 1.0 / (2 * CUTOFF), magic, ALU.mult, ALU.add).then_inc(steps, 1)
            dve.wait_ge(steps, 2)
            dve.tensor_scalar(turns[:, :], turns[:, :], magic, -2 * CUTOFF, ALU.subtract, ALU.mult).then_inc(steps, 1)
            dve.wait_ge(steps, 3)
            dve.tensor_tensor(u[:, :], wgt[:, :], turns[:, :], ALU.add).then_inc(steps, 1)
            dve.wait_ge(steps, 4)
            dve.scalar_tensor_tensor(u[:, :], u[:, :], -1.0, u[:, :], ALU.mult, ALU.max).then_inc(steps, 1)
            dve.wait_ge(sined, 1)
            dve.tensor_tensor(wgt[:, :], u[:, :], u[:, :], ALU.mult)

        @block.scalar
        def _(act):
            act.wait_ge(steps, 5)
            nc.scalar.activation(u[:, :], u[:, :], ACT.Sin, bias=half_pi[:, 0:1], scale=-PI / (2 * CUTOFF)).then_inc(sined, 1)


def layer1_edges(nc, sem, sbuf, src16, dst16, attr_cols, h1_parts, tabs, srcf, wgt, scat, basef, base, nwin,
                 pidx, half, ones3, zero, spare, bias3, nn1, nn2T, bank):
    f32, i32, i16, bf16 = mybir.dt.float32, mybir.dt.int32, mybir.dt.int16, mybir.dt.bfloat16
    ALU, ACT, ds = mybir.AluOpType, mybir.ActivationFunctionType, bass.ds
    attr = [sbuf(f"attr{h}", [GAUSS + 1, HE], f32) for h in range(2)]
    dstb = [sbuf(f"dstb{h}", [WIN, HE], i16) for h in range(2)]
    srcb = [sbuf(f"srcb1{h}", [P, HE], i16) for h in range(2)]
    h1w = [sbuf(f"h1w{h}", [WIN, 3 * D], bf16) for h in range(2)]
    sp1 = [sbuf(f"sp1_{h}", [P, HE], f32) for h in range(2)]
    sp2 = [sbuf(f"sp2_{h}", [P, HE], f32) for h in range(2)]
    hid = [sbuf(f"hid{h}", [P, HE], f32) for h in range(2)]
    filt = [sbuf(f"filt{h}", [P, HE], f32) for h in range(2)]
    ohT = [sbuf(f"ohT{h}", [WIN, HE], bf16) for h in range(2)]
    same = [sbuf(f"same{s}", [P, P], f32) for s in range(SUB)]
    rows = [sbuf(f"rows{h}", [P, HE], f32) for h in range(2)]
    sidx = [sbuf(f"sidx{h}", [P, HALF], i32) for h in range(2)]
    winp = sbuf("winp", [P, 1], f32)

    attr_in, dstb_in, srcb_in, h1w_in = ([sem(f"{n}_in{h}") for h in range(2)] for n in ("attr", "dstb", "srcb", "h1w"))
    up, down, taken, merged = sem("e_up"), sem("e_down"), sem("e_taken"), sem("e_merged")
    abs1, exp1, ln1, abs2, exp2, ln2 = (sem(f"e_{n}") for n in ("abs1", "exp1", "ln1", "abs2", "exp2", "ln2"))
    rows_set, sidx_set = sem("e_rows_set"), sem("e_sidx_set")
    oh_set, same_set, hid_set, filt_set, msg_set = (sem(f"e_{n}") for n in ("oh_set", "same_set", "hid_set", "filt_set", "msg_set"))
    tile_set, winp_set = sem("e_tile_set"), sem("e_winp_set")
    scattered = [sem(f"scattered{s}") for s in range(SUB)]
    passed, passed_sp, passed_dve = sem("e_passed_pool"), sem("e_passed_sp"), sem("e_passed_dve")

    with nc.Block() as block:
        @block.sync
        def _(sp):
            job, first = sp.alloc_register("sp_job1"), sp.alloc_register("sp_first1")
            sp.reg_mov(job, 0)
            with sp.Fori(0, T) as t:
                windows = sp.value_load(nwin[0:1, ds(t, 1)], min_val=1, max_val=-(-N // WIN))
                sp.reg_mov(first, sp.value_load(base[0:1, ds(t, 1)], min_val=0, max_val=NPAD - WIN))
                with sp.Fori(0, windows):
                    j = sp.snap(job, min_val=0, max_val=MAXJOBS)
                    node = sp.snap(first, min_val=0, max_val=NPAD - WIN)
                    for h in range(2):
                        sp.wait_ge(up, freed(j, h))
                        sp.dma_start(attr[h][:, :], attr_cols[:, ds(t * TE + h * HE, HE)]).then_inc(attr_in[h], 16)
                        wait_apart(sp, oh_set, freed(j, h), passed_sp)
                        sp.dma_start(dstb[h][:, :], dst16[ds(t, 1), h * HE:(h + 1) * HE].broadcast_to([WIN, HE])).then_inc(dstb_in[h], 16)
                        sp.wait_ge(same_set, freed(j, h))
                        sp.dma_start(srcb[h][:, :], src16[ds(t, 1), h * HE:(h + 1) * HE].broadcast_to([P, HE])).then_inc(srcb_in[h], 16)
                        sp.wait_ge(taken, freed(j, h))
                        sp.dma_start(h1w[h][:, :], h1_parts[ds(node, WIN), :]).then_inc(h1w_in[h], 16)
                    sp.reg_add(job, job, 1)
                    sp.reg_add(first, first, WIN)

        @block.tensor
        def _(pe):
            for s in (up, down, taken, merged):
                pe.sem_inc(s, 2)
            job = pe.alloc_register("pe_job1")
            pe.reg_mov(job, 0)
            with pe.Fori(0, T) as t:
                windows = pe.value_load(nwin[0:1, ds(t, 1)], min_val=1, max_val=-(-N // WIN))
                with pe.Fori(0, windows):
                    j = pe.snap(job, min_val=0, max_val=MAXJOBS)
                    for h in range(2):
                        pe.wait_ge(attr_in[h], 16 * (j + 1))
                        pe.wait_ge(hid_set, freed(j, h))
                        nc.tensor.matmul(bank[h][:, :], nn1[:, :], attr[h][:, :], start=True, stop=True).then_inc(up, 1)
                    for h in range(2):
                        pe.wait_ge(oh_set, done(j, h))
                        pe.wait_ge(h1w_in[h], 16 * (j + 1))
                        pe.wait_ge(msg_set, freed(j, h))
                        for s in range(HALF):
                            for k in range(3):
                                ins = nc.tensor.matmul(bank[4 + h][:, s * P:s * P + P], ohT[h][:, s * P:s * P + P],
                                                       h1w[h][:, k * D:k * D + D], start=(k == 0), stop=(k == 2))
                        ins.then_inc(taken, 1)
                        pe.wait_ge(filt_set, freed(j, h))
                        nc.tensor.matmul(bank[2 + h][:, :], ones3[:, :], bias3["nnb2"][:, :], start=True, stop=False)
                        pe.wait_ge(hid_set, done(j, h))
                        for s in range(HALF):
                            ins = nc.tensor.matmul(bank[2 + h][:, s * P:s * P + P], hid[h][:, s * P:s * P + P], nn2T[:, :],
                                                   start=False, stop=(s == HALF - 1))
                        ins.then_inc(down, 1)
                    for h in range(2):
                        pe.wait_ge(same_set, done(j, h))
                        pe.wait_ge(msg_set, done(j, h))
                        pe.wait_ge(rows_set, freed(j, h))
                        for s in range(HALF):
                            ins = nc.tensor.matmul(bank[6 + h][:, s * P:s * P + P], same[h * HALF + s][:, :],
                                                   filt[h][:, s * P:s * P + P], start=True, stop=True)
                        ins.then_inc(merged, 1)
                    pe.reg_add(job, job, 1)

        @block.scalar
        def _(act):
            nc.scalar.preload_act_table_set("natural_log_exp_and_others")
            for s in (abs1, exp1, ln1, abs2, exp2, ln2, rows_set, sidx_set):
                act.sem_inc(s, 2)
            job = act.alloc_register("act_job1")
            act.reg_mov(job, 0)
            with act.Fori(0, T) as t:
                windows = act.value_load(nwin[0:1, ds(t, 1)], min_val=1, max_val=-(-N // WIN))
                with act.Fori(0, windows):
                    j = act.snap(job, min_val=0, max_val=MAXJOBS)
                    for z0, buf, made, used, s_abs, s_exp, s_ln in (
                            (0, sp1, up, hid_set, abs1, exp1, ln1), (2, sp2, down, filt_set, abs2, exp2, ln2)):
                        for h in range(2):
                            act.wait_ge(made, done(j, h))
                            act.wait_ge(used, freed(j, h))
                            nc.scalar.activation(buf[h][:, :], bank[z0 + h][:, :], ACT.Abs).then_inc(s_abs, 1)
                        for h in range(2):
                            act.wait_ge(s_abs, done(j, h))
                            nc.scalar.activation(buf[h][:, :], buf[h][:, :], ACT.Exp, scale=-1.0).then_inc(s_exp, 1)
                        for h in range(2):
                            act.wait_ge(s_exp, done(j, h))
                            nc.scalar.activation(buf[h][:, :], buf[h][:, :], ACT.Ln, bias=half[:, 0:1], scale=0.5).then_inc(s_ln, 1)
                    for h in range(2):
                        for s in range(HALF):
                            act.wait_ge(scattered[h * HALF + s], 16 * (j + 1))
                        nc.scalar.activation(sidx[h][:, :], scat[:, ds(t * SUB + h * HALF, HALF)], ACT.Copy).then_inc(sidx_set, 1)
                        act.wait_ge(merged, done(j, h))
                        nc.scalar.activation(rows[h][:, :], bank[6 + h][:, :], ACT.Copy).then_inc(rows_set, 1)
                    act.reg_add(job, job, 1)

        @block.gpsimd
        def _(pool):
            for g in range(SUB):
                prime(pool, spare[16 + g:17 + g, :], scattered[g], zero)
            job = pool.alloc_register("pool_job1")
            pool.reg_mov(job, 0)
            with pool.Fori(0, T) as t:
                windows = pool.value_load(nwin[0:1, ds(t, 1)], min_val=1, max_val=-(-N // WIN))
                with pool.Fori(0, windows):
                    j = pool.snap(job, min_val=0, max_val=MAXJOBS)
                    for h in range(2):
                        pool.wait_ge(sidx_set, done(j, h))
                        for s in range(HALF):
                            g = h * HALF + s
                            pool.wait_ge(scattered[g], 16 * (j + 1))
                            wait_apart(pool, rows_set, done(j, h), passed)
                            pool.indirect_dma_start(tabs[g], bass.IndirectOffsetOnAxis(ap=sidx[h][:, s:s + 1], axis=0),
                                                    rows[h][:, s * P:s * P + P], None, compute_op=ALU.add).then_inc(scattered[g], 16)
                    pool.reg_add(job, job, 1)
            end = pool.snap(job, min_val=0, max_val=MAXJOBS)
            for g in range(SUB):
                pool.wait_ge(scattered[g], 16 * (end + 1))

        @block.vector
        def _(dve):
            for s in (oh_set, same_set, hid_set, filt_set, msg_set):
                dve.sem_inc(s, 2)
            dve.sem_inc(winp_set, 1)
            job = dve.alloc_register("dve_job1")
            dve.reg_mov(job, 0)
            with dve.Fori(0, T) as t:
                windows = dve.value_load(nwin[0:1, ds(t, 1)], min_val=1, max_val=-(-N // WIN))
                j0 = dve.snap(job, min_val=0, max_val=MAXJOBS)
                dve.wait_ge(winp_set, j0 + 1)
                dve.tensor_scalar(winp[:, :], pidx[:, :], basef[:, ds(t, 1)], float(WIN), ALU.add, ALU.subtract).then_inc(tile_set, 1)
                wait_apart(dve, tile_set, t + 1, passed_dve)
                with dve.Fori(0, windows):
                    j = dve.snap(job, min_val=0, max_val=MAXJOBS)
                    dve.wait_ge(winp_set, j + 1)
                    dve.tensor_single_scalar(winp[:, :], winp[:, :], float(WIN), ALU.add).then_inc(winp_set, 1)
                    dve.wait_ge(winp_set, j + 2)
                    for h in range(2):
                        dve.wait_ge(dstb_in[h], 16 * (j + 1))
                        dve.wait_ge(taken, freed(j, h))
                        dve.tensor_single_scalar(ohT[h][:, :], dstb[h][:, :], winp[0:WIN, 0:1], ALU.is_equal).then_inc(oh_set, 1)
                    for h in range(2):
                        dve.wait_ge(srcb_in[h], 16 * (j + 1))
                        dve.wait_ge(merged, freed(j, h))
                        for s in range(HALF):
                            at = ds(t * SUB + h * HALF + s, 1)
                            ins = dve.tensor_scalar(same[h * HALF + s][:, :], srcb[h][:, s * P:s * P + P], srcf[:, at], wgt[:, at],
                                                    ALU.is_equal, ALU.mult)
                        ins.then_inc(same_set, 1)
                    for h in range(2):
                        dve.wait_ge(ln1, done(j, h))
                        dve.wait_ge(down, freed(j, h))
                        dve.scalar_tensor_tensor(hid[h][:, :], bank[h][:, :], 0.0, sp1[h][:, :], ALU.max, ALU.add).then_inc(hid_set, 1)
                    for h in range(2):
                        dve.wait_ge(ln2, done(j, h))
                        dve.wait_ge(merged, freed(j, h))
                        dve.scalar_tensor_tensor(filt[h][:, :], bank[2 + h][:, :], 0.0, sp2[h][:, :], ALU.max, ALU.add).then_inc(filt_set, 1)
                    for h in range(2):
                        dve.wait_ge(filt_set, done(j, h))
                        dve.wait_ge(taken, done(j, h))
                        dve.tensor_tensor(filt[h][:, :], filt[h][:, :], bank[4 + h][:, :], ALU.mult).then_inc(msg_set, 1)
                    dve.reg_add(job, job, 1)


def layer1_nodes(nc, sem, sbuf, x1_d, tabs, lin2T, bias3, ones3, ident, eps, zero, spare, bank, out):
    f32 = mybir.dt.float32
    ALU, ACT, ds = mybir.AluOpType, mybir.ActivationFunctionType, bass.ds
    tab = [[sbuf(f"tab{h}_{k}", [P, 2, D], f32) for k in range(NTAB)] for h in range(2)]
    h2T = [sbuf(f"f_h2T{h}", [P, NH], f32) for h in range(2)]
    x1 = [sbuf(f"f_x1{h}", [P, 2, D], f32) for h in range(2)]
    y = [sbuf(f"f_y{h}", [P, 2, D], f32) for h in range(2)]
    o = [sbuf(f"f_o{h}", [P, 2, D], f32) for h in range(2)]
    stats = [sbuf(f"f_stats{h}", [P, 2, 6], f32) for h in range(2)]
    mean_var = [sbuf(f"f_mv{h}", [P, 2, 2], f32) for h in range(2)]
    std = [sbuf(f"f_std{h}", [P, 2], f32) for h in range(2)]
    rstd = [sbuf(f"f_rstd{h}", [P, 2], f32) for h in range(2)]
    var_set, std_set, passed = sem("f_var_set"), sem("f_std_set"), sem("f_passed")
    loaded = [sem(f"f_loaded{h}") for h in range(2)]
    stored = [sem(f"f_stored{h}") for h in range(2)]
    turned, turned_out, lin, steps, o_set = (sem(f"f_{n}") for n in ("turned", "turned_out", "lin", "steps", "o_set"))
    nload = 16 * (NTAB + 1)

    with nc.Block() as block:
        @block.sync
        def _(sp):
            with sp.Fori(0, NCH) as c:
                for h in range(2):
                    at = ds(c * CHUNK + h * NH, NH)
                    sp.wait_ge(turned, freed(c, h))
                    sp.wait_ge(o_set, freed(c, h))
                    for k in range(NTAB):
                        sp.dma_start(tab[h][k][:, :, :], tabs[k][at, :].rearrange("(i p) d -> p i d", p=P)).then_inc(loaded[h], 16)
                    sp.dma_start(x1[h][:, :, :], x1_d[at, :].rearrange("(i p) d -> p i d", p=P)).then_inc(loaded[h], 16)

        @block.tensor
        def _(pe):
            for s in (turned, lin):
                pe.sem_inc(s, 2)
            with pe.Fori(0, NCH) as c:
                for h in range(2):
                    pe.wait_ge(loaded[h], nload * (c + 1))
                    pe.wait_ge(turned_out, freed(c, h))
                    for i in range(2):
                        for k in range(NTAB):
                            ins = nc.tensor.matmul(bank[h][:, i * P:i * P + P], tab[h][k][:, i, :], ident[:, :],
                                                   start=(k == 0), stop=(k == NTAB - 1))
                    ins.then_inc(turned, 1)
                for h in range(2):
                    pe.wait_ge(turned_out, done(c, h))
                    pe.wait_ge(o_set, freed(c, h))
                    nc.tensor.matmul(bank[2 + h][:, 0:NH], ones3[:, :], bias3["lin2b"][:, 0:NH], start=True, stop=False)
                    for i in range(2):
                        ins = nc.tensor.matmul(bank[2 + h][:, i * P:i * P + P], h2T[h][:, i * P:i * P + P], lin2T[:, :],
                                               start=False, stop=(i == 1))
                    ins.then_inc(lin, 1)

        @block.scalar
        def _(act):
            act.sem_inc(turned_out, 2)
            act.sem_inc(std_set, 2)
            for h in range(2):
                prime(act, spare[24 + h:25 + h, :], stored[h], zero)
            with act.Fori(0, NCH) as c:
                for h in range(2):
                    act.wait_ge(turned, done(c, h))
                    act.wait_ge(lin, freed(c, h))
                    nc.scalar.activation(h2T[h][:, :], bank[h][:, 0:NH], ACT.Copy).then_inc(turned_out, 1)
                for h in range(2):
                    act.wait_ge(var_set, done(c, h))
                    nc.scalar.activation(std[h][:, :], mean_var[h][:, :, 1], ACT.Sqrt, bias=eps[:, 0:1]).then_inc(std_set, 1)
                for h in range(2):
                    act.wait_ge(o_set, done(c, h))
                    act.dma_start(out[ds(c * CHUNK + h * NH, NH), :].rearrange("(i p) d -> p i d", p=P), o[h][:, :, :]).then_inc(stored[h], 16)
            for h in range(2):
                act.wait_ge(stored[h], 16 * (NCH + 1))

        @block.vector
        def _(dve):
            dve.sem_inc(o_set, 2)
            dve.sem_inc(var_set, 2)
            with dve.Fori(0, NCH) as c:
                for h in range(2):
                    dve.wait_ge(lin, done(c, h))
                    dve.wait_ge(loaded[h], nload * (c + 1))
                    dve.wait_ge(stored[h], 16 * (c + 1))
                    dve.tensor_tensor(y[h][:, :, :], bank[2 + h][:, 0:NH].rearrange("p (i d) -> p i d", i=2),
                                      x1[h][:, :, :], ALU.add).then_inc(steps, 1)
                    layer_norm_stats(dve, steps, passed, LN_STEPS * c + 5 * h, y[h], stats[h], mean_var[h])
                    dve.wait_ge(steps, LN_STEPS * c + 5 * h + 5)
                    dve.sem_inc(var_set, 1)
                for h in range(2):
                    dve.wait_ge(std_set, done(c, h))
                    layer_norm_apply(dve, steps, passed, LN_STEPS * c + 10 + 3 * h, y[h], mean_var[h], std[h], rstd[h], o[h])
                    dve.wait_ge(steps, LN_STEPS * c + 13 + 3 * h)
                    dve.sem_inc(o_set, 1)


_OUTS = [((NPAD, D), "float32")]


def kernel(x, src, dst, edge_attr_50, edge_weight, L0_gnn_W1, L0_gnn_b1, L0_gnn_W2, L0_gnn_b2,
           L1_gnn_lin1_w, L1_gnn_nn_w1, L1_gnn_nn_b1, L1_gnn_nn_w2, L1_gnn_nn_b2, L1_gnn_lin2_w, L1_gnn_lin2_b):
    import numpy as np
    import concourse.bacc as bacc
    from concourse.bass_utils import run_bass_kernel_spmd

    x, src, dst, attr, w = (np.asarray(a) for a in (x, src, dst, edge_attr_50, edge_weight))
    pad = EPAD - E
    src = np.concatenate([src, np.arange(N, N + pad, dtype=src.dtype)])
    dst = np.concatenate([dst, np.full(pad, N - 1, dst.dtype)])
    w = np.concatenate([w, np.zeros(pad, w.dtype)])
    xp = np.zeros((NPAD, D), x.dtype)
    xp[:N] = x
    at = np.zeros((GAUSS + 1, EPAD), attr.dtype)
    at[:GAUSS, :E] = attr.T
    at[GAUSS] = 1

    def cols(a):
        return np.ascontiguousarray(a.reshape(T * SUB, P).T)

    row = lambda a: np.asarray(a).reshape(1, D)
    tr = lambda a: np.ascontiguousarray(np.asarray(a).T)
    ins = {
        "x_rows": xp, "x_cols": tr(xp), "src_cols": cols(src), "dst_cols": cols(dst), "w_cols": cols(w),
        "src_rows": src.reshape(T, TE), "dst_rows": dst.reshape(T, TE), "attr_cols": at,
        "W1": np.asarray(L0_gnn_W1), "b1": np.asarray(L0_gnn_b1).reshape(D, 1), "W2": np.asarray(L0_gnn_W2),
        "b2": row(L0_gnn_b2), "lin1T": tr(L1_gnn_lin1_w),
        "nn1T": np.concatenate([tr(L1_gnn_nn_w1), row(L1_gnn_nn_b1)]), "nn2T": tr(L1_gnn_nn_w2),
        "nnb2": row(L1_gnn_nn_b2), "lin2T": tr(L1_gnn_lin2_w), "lin2b": row(L1_gnn_lin2_b),
    }
    nc = bacc.Bacc("TRN2", target_bir_lowering=False, num_devices=1)
    args = {n: nc.dram_tensor(n, a.shape, mybir.dt.from_np(a.dtype), kind="ExternalInput").ap() for n, a in ins.items()}
    out = nc.dram_tensor("out", (NPAD, D), mybir.dt.float32, kind="ExternalOutput").ap()
    edge_network_kernel(nc, out=out, **args)
    r = run_bass_kernel_spmd(nc, [ins], core_ids=[0])
    return r.results[0]["out"][:N]
```

```python
from contextlib import ExitStack

import concourse.bass as bass
from concourse import mybir

D = 128
P = 128
N = 12500
E = 412500
GAUSS = 50
CHUNK = 512
NH = CHUNK // 2
NPAD = -(-N // CHUNK) * CHUNK
SUB = 8
NCH = NPAD // CHUNK
HALF = SUB // 2
HE = HALF * P
TE = SUB * P
T = -(-E // TE)
EPAD = T * TE
NGRP = -(-T // P)
WIN = 64
SPARE = NPAD
TROWS = NPAD + P
NTAB = SUB
MAXJOBS = T * (-(-N // WIN))
LN_EPS = 1e-5
CREDIT = 4
CUTOFF = 10.0
PI = 3.141592653589793
LN2 = 0.6931471805599453
SURE = 40.0


def edge_network_kernel(nc, x_rows, x_cols, src_cols, dst_cols, w_cols, src_rows, dst_rows,
                        attr_cols, W1, b1, W2, b2, lin1T, nn1T, nn2T, nnb2, lin2T, lin2b, out):
    f32, i32, i16, bf16 = mybir.dt.float32, mybir.dt.int32, mybir.dt.int16, mybir.dt.bfloat16
    ALU = mybir.AluOpType
    ACT = mybir.ActivationFunctionType
    AX = mybir.AxisListType
    ds = bass.ds

    ctx = ExitStack()
    with ctx:
        def sb(name, shape, dt):
            return ctx.enter_context(nc.sbuf_tensor(name, shape, dt))

        def sem(name):
            return ctx.enter_context(nc.semaphore(name))

        src16 = nc.dram_tensor("src16", [T, TE], i16, kind="Internal").ap()
        dst16 = nc.dram_tensor("dst16", [T, TE], i16, kind="Internal").ap()
        base_d = nc.dram_tensor("base_d", [NGRP * P, 1], i32, kind="Internal").ap()
        nwin_d = nc.dram_tensor("nwin_d", [NGRP * P, 1], i32, kind="Internal").ap()
        x1_d = nc.dram_tensor("x1_d", [NPAD, D], f32, kind="Internal").ap()
        h1_parts = nc.dram_tensor("h1_parts", [NPAD, 3 * D], bf16, kind="Internal").ap()
        spare = nc.dram_tensor("spare", [32, 16], f32, kind="Internal").ap()
        tabs = [nc.dram_tensor(f"sum_table{k}", [TROWS, D], f32, kind="Internal").ap()
                for k in range(NTAB)]

        srcf = sb("srcf", [P, T * SUB], f32)
        dstf = sb("dstf", [P, T * SUB], f32)
        wgt = sb("wgt", [P, T * SUB], f32)
        repeats = sb("repeats", [P, T * SUB], f32)
        scat = sb("scat", [P, T * SUB], i32)
        base = sb("base", [P, T + 1], i32)
        basef = sb("basef", [P, T], f32)
        nwin = sb("nwin", [P, T + 1], i32)
        ident = sb("ident", [P, P], f32)
        tri = sb("tri", [P, P], f32)
        cols = sb("cols", [P, WIN], f32)
        pidx = sb("pidx", [P, 1], f32)
        spare_row = sb("spare_row", [P, 1], f32)
        eps = sb("eps", [P, 1], f32)
        half = sb("half", [P, 1], f32)
        ones3 = sb("ones3", [3, P], bf16)
        bias3 = {n: sb(f"bias3_{n}", [3, HE], bf16) for n in ("b2", "nnb2", "lin2b")}
        zero = sb("zero", [P, 512], f32)
        w_sb = {n: sb(f"w_{n}", [P, D], f32) for n in ("W1", "W2", "lin1T", "nn2T", "lin2T")}
        nn1 = sb("nn1", [GAUSS + 1, D], f32)
        b1c = sb("b1c", [P, 1], f32)
        bank = [ctx.enter_context(nc.psum_tensor(f"bank{i}", [P, 512], f32)) for i in range(8)]

        with ExitStack() as c0:
            def sb0(name, shape, dt):
                return c0.enter_context(nc.sbuf_tensor(name, shape, dt))

            rows_i = sb0("rows_i", [P, NGRP, 2, TE], i32)
            rows_h = sb0("rows_h", [P, NGRP, 2, TE], i16)
            cols_i = sb0("cols_i", [P, 2, T * SUB], i32)
            least = sb0("least", [P, NGRP], i32)
            most = sb0("most", [P, NGRP], i32)
            brow = sb0("brow", [1, 3, D], f32)
            bpart = sb0("bpart", [1, 3, 3, 4, D], bf16)
            brest = sb0("brest", [1, 2, 3, D], f32)
            s_rows, s_cols, s_w = sem("rows_loaded"), sem("cols_loaded"), sem("weights_loaded")
            s_brow, s_const, s_pool = sem("bias_rows"), sem("consts"), sem("pool_consts")
            s_win, s_half, s_split = sem("windows"), sem("halved"), sem("split_step")
            s_st, s_tab, s_b3, s_zero = sem("scratch_stored"), sem("table_loaded"), sem("bias_moved"), sem("zeroed")
            s_fin, s_dv = sem("setup_cols"), sem("window_steps")
            s_less = sem("bias_less_ln2")
            g = [min(P, T - P * i) for i in range(NGRP)]

            with nc.Block() as block:
                @block.sync
                def _(sp):
                    for i in range(NGRP):
                        sp.dma_start(rows_i[0:g[i], i, 0, :], dst_rows[P * i:P * i + g[i], :]).then_inc(s_rows, 16)
                        sp.dma_start(rows_i[0:g[i], i, 1, :], src_rows[P * i:P * i + g[i], :]).then_inc(s_rows, 16)
                    for n, v in (("W1", W1), ("W2", W2), ("lin1T", lin1T), ("nn2T", nn2T), ("lin2T", lin2T)):
                        sp.dma_start(w_sb[n][:, :], v).then_inc(s_w, 16)
                    sp.dma_start(nn1[:, :], nn1T).then_inc(s_w, 16)
                    sp.dma_start(b1c[:, :], b1).then_inc(s_w, 16)
                    sp.wait_ge(s_split, 5)
                    for i, n in enumerate(("b2", "nnb2", "lin2b")):
                        for k in range(3):
                            sp.dma_start(bias3[n][k:k + 1, :], bpart[0:1, k, i, :, :].rearrange("o a d -> o (a d)")).then_inc(s_b3, 16)
                    sp.wait_ge(s_win, 1)
                    for i in range(NGRP):
                        sp.dma_start(base_d[P * i:P * i + g[i], :], least[0:g[i], i:i + 1]).then_inc(s_st, 16)
                        sp.dma_start(nwin_d[P * i:P * i + g[i], :], most[0:g[i], i:i + 1]).then_inc(s_st, 16)
                    sp.wait_ge(s_half, NGRP)
                    for i in range(NGRP):
                        sp.dma_start(dst16[P * i:P * i + g[i], :], rows_h[0:g[i], i, 0, :]).then_inc(s_st, 16)
                        sp.dma_start(src16[P * i:P * i + g[i], :], rows_h[0:g[i], i, 1, :]).then_inc(s_st, 16)
                    sp.wait_ge(s_st, 16 * 4 * NGRP)
                    sp.dma_start(base[:, 0:T], base_d[0:T, :].rearrange("t o -> o t").broadcast_to([P, T])).then_inc(s_tab, 16)
                    sp.dma_start(nwin[:, 0:T], nwin_d[0:T, :].rearrange("t o -> o t").broadcast_to([P, T])).then_inc(s_tab, 16)
                    sp.wait_ge(s_w, 16 * 7)
                    sp.wait_ge(s_b3, 16 * 9)
                    sp.wait_ge(s_tab, 32)

                @block.scalar
                def _(act):
                    act.dma_start(cols_i[:, 0, :], src_cols).then_inc(s_cols, 16)
                    act.dma_start(cols_i[:, 1, :], dst_cols).then_inc(s_cols, 16)
                    act.dma_start(wgt[:, :], w_cols).then_inc(s_cols, 16)
                    for i, v in enumerate((b2, nnb2, lin2b)):
                        act.dma_start(brow[0:1, i, :], v).then_inc(s_brow, 16)
                    act.wait_ge(s_cols, 48)
                    nc.scalar.activation(srcf[:, :], cols_i[:, 0, :], ACT.Copy).then_inc(s_fin, 1)
                    nc.scalar.activation(dstf[:, :], cols_i[:, 1, :], ACT.Copy).then_inc(s_fin, 1)

                @block.gpsimd
                def _(pool):
                    pool.memset(zero[:, :], 0.0).then_inc(s_zero, 1)
                    pool.memset(ident[:, :], 0.0).then_inc(s_pool, 1)
                    pool.memset(tri[:, :], 1.0).then_inc(s_pool, 1)
                    pool.memset(ones3[:, :], 1.0).then_inc(s_pool, 1)
                    pool.memset(half[:, :], 0.5).then_inc(s_pool, 1)
                    pool.memset(nwin[:, T:T + 1], 1).then_inc(s_pool, 1)
                    pool.memset(base[:, T:T + 1], 0).then_inc(s_pool, 1)
                    pool.memset(eps[:, :], LN_EPS).then_inc(s_pool, 1)
                    pool.iota(cols[:, :], pattern=[[1, WIN]], base=0, channel_multiplier=0,
                              allow_small_or_imprecise_dtypes=True).then_inc(s_pool, 1)
                    pool.iota(pidx[:, :], pattern=[[0, 1]], base=0, channel_multiplier=1,
                              allow_small_or_imprecise_dtypes=True).then_inc(s_pool, 1)
                    pool.iota(spare_row[:, :], pattern=[[0, 1]], base=SPARE, channel_multiplier=1,
                              allow_small_or_imprecise_dtypes=True).then_inc(s_pool, 1)
                    pool.wait_ge(s_pool, 10)
                    pool.affine_select(out=ident[:, :], in_=ident[:, :], compare_op=ALU.not_equal, fill=1.0,
                                       base=0, pattern=[[-1, P]], channel_multiplier=1)
                    pool.affine_select(out=tri[:, :], in_=tri[:, :], compare_op=ALU.is_gt, fill=0.0,
                                       base=0, pattern=[[-1, P]], channel_multiplier=1)

                @block.vector
                def _(dve):
                    dve.wait_ge(s_rows, 32 * NGRP)
                    for i in range(NGRP):
                        dve.tensor_copy(rows_h[0:g[i], i, :, :], rows_i[0:g[i], i, :, :]).then_inc(s_half, 1)
                    for i in range(NGRP):
                        dve.tensor_reduce(least[0:g[i], i:i + 1], rows_i[0:g[i], i, 0, :], axis=AX.X, op=ALU.min).then_inc(s_dv, 1)
                        dve.tensor_reduce(most[0:g[i], i:i + 1], rows_i[0:g[i], i, 0, :], axis=AX.X, op=ALU.max).then_inc(s_dv, 1)
                    at = 2 * NGRP
                    for op in (lambda a, b: dve.tensor_tensor(a, a, b, ALU.subtract),
                               lambda a, b: dve.tensor_single_scalar(a, a, 6, ALU.arith_shift_right),
                               lambda a, b: dve.tensor_single_scalar(a, a, 1, ALU.add)):
                        dve.wait_ge(s_dv, at)
                        for i in range(NGRP):
                            op(most[0:g[i], i:i + 1], least[0:g[i], i:i + 1]).then_inc(s_dv, 1)
                        at += NGRP
                    dve.wait_ge(s_dv, at)
                    dve.sem_inc(s_win, 1)
                    dve.wait_ge(s_brow, 48)
                    dve.wait_ge(s_w, 16 * 7)
                    for b in (nn1[0:1, :], brow[:, 1, :]):
                        dve.tensor_single_scalar(b, b, LN2, ALU.subtract).then_inc(s_less, 1)
                    dve.wait_ge(s_less, 2)
                    hi, mid, lo = (bpart[0:1, k, :, 0, :] for k in range(3))
                    dve.tensor_copy(hi, brow[:, :, :]).then_inc(s_split, 1)
                    dve.wait_ge(s_split, 1)
                    dve.tensor_tensor(brest[:, 0, :, :], brow[:, :, :], hi, ALU.subtract).then_inc(s_split, 1)
                    dve.wait_ge(s_split, 2)
                    dve.tensor_copy(mid, brest[:, 0, :, :]).then_inc(s_split, 1)
                    dve.wait_ge(s_split, 3)
                    dve.tensor_tensor(lo, brest[:, 0, :, :], mid, ALU.subtract).then_inc(s_split, 1)
                    dve.wait_ge(s_split, 4)
                    dve.tensor_copy(bpart[:, :, :, 1:4, :].rearrange("o k i a d -> o (k i) a d"),
                                    bpart[:, :, :, 0:1, :].rearrange("o k i a d -> o (k i) a d")
                                    .broadcast_to([1, 9, 3, D])).then_inc(s_split, 1)
                    dve.wait_ge(s_tab, 32)
                    dve.tensor_copy(basef[:, :], base[:, 0:T])
                    dve.wait_ge(s_pool, 10)
                    dve.tensor_single_scalar(pidx[WIN:P, :], pidx[WIN:P, :], float(WIN), ALU.subtract)

        with ExitStack() as c1:
            def sb1(name, shape, dt):
                return c1.enter_context(nc.sbuf_tensor(name, shape, dt))

            aggT = sb1("aggT", [D, NPAD], f32)
            with ExitStack() as c2:
                def sb2(name, shape, dt):
                    return c2.enter_context(nc.sbuf_tensor(name, shape, dt))

                gidx = [sb2(f"gidx{h}", [P, HALF], i32) for h in range(2)]
                xg = [sb2(f"xg{s}", [P, D], f32) for s in range(SUB)]
                onehot = [sb2(f"onehot{h}", [P, HALF, WIN], f32) for h in range(2)]
                srcb = [sb2(f"srcb{h}", [P, HE], i16) for h in range(2)]
                eq = [sb2(f"eq{s}", [P, P], bf16) for s in range(SUB)]
                dup = sb2("dup", [P, SUB], f32)
                rel = sb2("rel", [P, SUB], f32)
                x_loaded, tables_zero = sem("x_loaded"), sem("tables_zero")
                gidx_ready = [sem(f"gidx_ready{h}") for h in range(2)]
                gathered = [sem(f"gathered{s}") for s in range(SUB)]
                summed = sem("summed")
                onehot_ready = sem("onehot_ready")
                srcb_ready = [sem(f"srcb_ready{h}") for h in range(2)]
                dups_done = sem("dups_done")
                flushed = sem("flushed")
                rel_set = sem("rel_set")
                passed, scat_set, hot_set = sem("passed_pool"), sem("repeats_kept"), sem("hot_set")

                with nc.Block() as block:
                    @block.sync
                    def _(sp):
                        sp.dma_start(aggT[:, :], x_cols).then_inc(x_loaded, 16)
                        jobs = TileTable(sp, "sp0", nwin)
                        with sp.Fori(0, T) as t:
                            windows = jobs.windows()
                            with sp.Fori(0, windows):
                                j = jobs.number()
                                jobs.read_ahead(t)
                                for h in range(2):
                                    sp.wait_ge(dups_done, freed(j, h))
                                    sp.dma_start(srcb[h][:, :], src16[ds(t, 1), h * HE:(h + 1) * HE]
                                                 .broadcast_to([P, HE])).then_inc(srcb_ready[h], 16)
                                jobs.step()
                        sp.wait_ge(x_loaded, 16)

                    @block.scalar
                    def _(act):
                        for k in range(NTAB):
                            if k:
                                act.dma_start(tabs[k][0:NPAD, :].rearrange("(p a) d -> p (a d)", p=P)
                                              .rearrange("p (r c) -> p r c", c=512),
                                              zero[:, :].rearrange("p (o c) -> p o c", o=1)
                                              .broadcast_to([P, NPAD * D // P // 512, 512])).then_inc(tables_zero, 16)
                            act.dma_start(tabs[k][NPAD:TROWS, :], zero[:, 0:D]).then_inc(tables_zero, 16)
                        jobs = TileTable(act, "act0", nwin)
                        with act.Fori(0, T) as t:
                            windows = jobs.windows()
                            with act.Fori(0, windows):
                                j = jobs.number()
                                jobs.read_ahead(t)
                                for h in range(2):
                                    for s in range(HALF * h, HALF * h + HALF):
                                        act.wait_ge(gathered[s], 16 * (j + 1))
                                    nc.scalar.activation(gidx[h][:, :], srcf[:, ds(t * SUB + HALF * h, HALF)],
                                                         ACT.Copy).then_inc(gidx_ready[h], 1)
                                jobs.step()
                        act.wait_ge(tables_zero, 16 * (2 * NTAB - 1))

                    @block.gpsimd
                    def _(pool):
                        for s in range(SUB):
                            prime(pool, spare[s:s + 1, :], gathered[s], zero)
                        jobs = TileTable(pool, "pool0", nwin)
                        with pool.Fori(0, T) as t:
                            windows = jobs.windows()
                            with pool.Fori(0, windows):
                                j = jobs.number()
                                for s in range(SUB):
                                    if s == HALF + 1:
                                        jobs.read_ahead(t)
                                    if s % HALF == 0:
                                        pool.wait_ge(gidx_ready[s // HALF], j + 1)
                                    wait_apart(pool, summed, SUB * j + s + 1, passed)
                                    pool.indirect_dma_start(
                                        xg[s][:, :], None, x_rows,
                                        bass.IndirectOffsetOnAxis(ap=gidx[s // HALF][:, s % HALF:s % HALF + 1], axis=0),
                                    ).then_inc(gathered[s], 16)
                                jobs.step()

                    @block.tensor
                    def _(pe):
                        pe.sem_inc(summed, SUB)
                        jobs = TileTable(pe, "pe0", nwin)
                        with pe.Fori(0, T) as t:
                            windows = jobs.windows()
                            with pe.Fori(0, windows):
                                j = jobs.number()
                                for s in range(SUB):
                                    h = s // HALF
                                    if s == HALF:
                                        jobs.read_ahead(t)
                                    if s % HALF == 0:
                                        pe.wait_ge(flushed, freed(j, h))
                                    pe.wait_ge(gathered[s], 16 * (j + 2))
                                    if s % HALF == 0:
                                        pe.wait_ge(onehot_ready, 2 * j + h + 1)
                                    nc.tensor.matmul(bank[h][:, 0:WIN], xg[s][:, :], onehot[h][:, s % HALF, :],
                                                     start=(s % HALF == 0), stop=(s % HALF == HALF - 1)).then_inc(summed, 1)
                                jobs.step()

                    @block.vector
                    def _(dve):
                        dve.sem_inc(dups_done, CREDIT)
                        dve.sem_inc(flushed, CREDIT)
                        dve.sem_inc(scat_set, 1)
                        cols3 = cols[:, :].rearrange("p (o w) -> p o w", o=1)
                        dve.wait_ge(x_loaded, 16)
                        jobs = TileTable(dve, "dve0", nwin, base)
                        with dve.Fori(0, T) as t:
                            here = dve.snap(t * SUB, min_val=0, max_val=(T - 1) * SUB)
                            dve.tensor_single_scalar(rel[:, :], dstf[:, ds(here, SUB)], basef[:, ds(t, 1)], ALU.subtract).then_inc(rel_set, 1)
                            windows = jobs.windows()
                            with dve.Fori(0, windows):
                                j = jobs.number()
                                node = jobs.first_node()
                                dve.wait_ge(rel_set, t + j + 1)
                                for h in range(2):
                                    dve.wait_ge(summed, SUB * j + HALF * (h + 1))
                                    dve.tensor_tensor(onehot[h][:, :, :], cols3.broadcast_to([P, HALF, WIN]),
                                                      rel[:, h * HALF:(h + 1) * HALF].rearrange("p (s o) -> p s o", o=1).broadcast_to([P, HALF, WIN]),
                                                      ALU.is_equal).then_inc(hot_set, 1)
                                for h in range(2):
                                    dve.wait_ge(hot_set, 2 * j + h + 1)
                                    dve.tensor_tensor(onehot[h][:, :, :], onehot[h][:, :, :],
                                                      wgt[:, ds(here + h * HALF, HALF)].rearrange("p (s o) -> p s o", o=1).broadcast_to([P, HALF, WIN]),
                                                      ALU.mult).then_inc(onehot_ready, 1)
                                jobs.read_ahead(t)
                                dve.wait_ge(onehot_ready, 2 * j + 2)
                                dve.tensor_single_scalar(rel[:, :], rel[:, :], float(WIN), ALU.subtract).then_inc(rel_set, 1)
                                dve.wait_ge(scat_set, j + 1)
                                for s in range(SUB):
                                    h, o = s // HALF, (s % HALF) * P
                                    if s % HALF == 0:
                                        dve.wait_ge(srcb_ready[h], 16 * (j + 1))
                                    ins = dve.scalar_tensor_tensor(eq[s][:, :], srcb[h][:, o:o + P], srcf[:, ds(here + s, 1)], tri[:, :],
                                                                   ALU.is_equal, ALU.mult, accum_out=dup[:, s:s + 1])
                                    if s % HALF == HALF - 1:
                                        ins.then_inc(dups_done, 1)
                                dve.wait_ge(dups_done, done(j, 1))
                                dve.tensor_copy(repeats[:, ds(here, SUB)], dup[:, :]).then_inc(scat_set, 1)
                                for h in range(2):
                                    dve.wait_ge(summed, SUB * (j + 1) + HALF * (h + 1))
                                    dve.wait_ge(flushed, freed(j, h) + 1)
                                    dve.tensor_tensor(aggT[:, ds(node, WIN)], aggT[:, ds(node, WIN)], bank[h][:, 0:WIN],
                                                      ALU.add).then_inc(flushed, 1)
                                jobs.step()

            layer0_nodes(nc, sem, sb1, aggT, x_rows, x1_d, h1_parts, tabs[0], w_sb, b1c, bias3, ones3, ident, eps, zero, spare, bank)

        with ExitStack() as c3:
            layer1_edge_tables(nc, sem, lambda n, s, d: c3.enter_context(nc.sbuf_tensor(n, s, d)), wgt, srcf, repeats, spare_row, scat)
        with ExitStack() as c4:
            layer1_edges(nc, sem, lambda n, s, d: c4.enter_context(nc.sbuf_tensor(n, s, d)), src16, dst16, attr_cols,
                         h1_parts, tabs, srcf, wgt, scat, basef, base, nwin, pidx, spare_row, half,
                         ones3, zero, spare, bias3, nn1, w_sb["nn2T"], bank)
        with ExitStack() as c5:
            layer1_nodes(nc, sem, lambda n, s, d: c5.enter_context(nc.sbuf_tensor(n, s, d)), x1_d, tabs, w_sb["lin2T"],
                         bias3, ones3, ident, eps, zero, spare, bank, out)


def done(c, h):
    return 2 * c + h + CREDIT + 1


def freed(c, h):
    return 2 * c + h + CREDIT - 1


class TileTable:

    def __init__(self, engine, name, nwin, base=None):
        self.engine, self.nwin, self.base = engine, nwin, base
        self.job, self.count, self.next_count, self.node, self.next_node = (
            engine.alloc_register(f"{name}_{r}") for r in ("job", "count", "next_count", "node", "next_node"))
        engine.reg_mov(self.job, 0)
        engine.reg_load(self.next_count, nwin[0:1, 0:1])
        if base is not None:
            engine.reg_load(self.next_node, base[0:1, 0:1])

    def windows(self):
        self.engine.reg_mov(self.count, self.next_count)
        if self.base is not None:
            self.engine.reg_mov(self.node, self.next_node)
        return self.engine.snap(self.count, min_val=1, max_val=-(-N // WIN))

    def number(self):
        return self.engine.snap(self.job, min_val=0, max_val=MAXJOBS)

    def first_node(self):
        return self.engine.snap(self.node, min_val=0, max_val=NPAD - WIN)

    def read_ahead(self, t):
        self.engine.reg_load(self.next_count, self.nwin[0:1, bass.ds(t + 1, 1)])
        if self.base is not None:
            self.engine.reg_load(self.next_node, self.base[0:1, bass.ds(t + 1, 1)])

    def step(self):
        self.engine.reg_add(self.job, self.job, 1)
        if self.base is not None:
            self.engine.reg_add(self.node, self.node, WIN)


def prime(engine, spare, semaphore, zero):
    engine.dma_start(spare, zero[0:1, 0:16]).then_inc(semaphore, 16)


def wait_apart(engine, semaphore, value, passed):
    engine.wait_ge(semaphore, value)
    engine.sem_inc(passed, 1)


LN_STEPS = 16


def layer_norm_stats(dve, steps, passed, at, y, stats, mean_var):
    wait_apart(dve, steps, at + 1, passed)
    for i in range(2):
        dve.bn_stats(stats[:, i, :], y[:, i, :]).then_inc(steps, 1)
    wait_apart(dve, steps, at + 3, passed)
    for i in range(2):
        dve.bn_aggr(mean_var[:, i, :], stats[:, i, :]).then_inc(steps, 1)


def layer_norm_apply(dve, steps, passed, at, y, mean_var, std, rstd, rows):
    ALU = mybir.AluOpType
    dve.reciprocal(rstd[:, :], std[:, :]).then_inc(steps, 1)
    wait_apart(dve, steps, at + 1, passed)
    for i in range(2):
        dve.tensor_scalar(rows[:, i, :], y[:, i, :], mean_var[:, i, 0:1], rstd[:, i:i + 1],
                          ALU.subtract, ALU.mult).then_inc(steps, 1)


def layer0_nodes(nc, sem, sbuf, aggT, x_rows, x1_d, h1_parts, tab0, w_sb, b1c, bias3, ones3, ident, eps, zero, spare, bank):
    f32, bf16 = mybir.dt.float32, mybir.dt.bfloat16
    ALU, ACT, ds = mybir.AluOpType, mybir.ActivationFunctionType, bass.ds
    hidT = [sbuf(f"n_hidT{h}", [P, NH], f32) for h in range(2)]
    xr = [sbuf(f"n_xr{h}", [P, 2, D], f32) for h in range(2)]
    y = [sbuf(f"n_y{h}", [P, 2, D], f32) for h in range(2)]
    x1 = [sbuf(f"n_x1{h}", [P, 2, D], f32) for h in range(2)]
    x1T = [sbuf(f"n_x1T{h}", [P, NH], f32) for h in range(2)]
    h1 = [sbuf(f"n_h1{h}", [P, 2, D], f32) for h in range(2)]
    parts = [sbuf(f"n_parts{h}", [P, 2, 3, D], bf16) for h in range(2)]
    rest = [sbuf(f"n_rest{h}", [P, 2, 2, D], f32) for h in range(2)]
    stats = [sbuf(f"n_stats{h}", [P, 2, 6], f32) for h in range(2)]
    mean_var = [sbuf(f"n_mv{h}", [P, 2, 2], f32) for h in range(2)]
    std = [sbuf(f"n_std{h}", [P, 2], f32) for h in range(2)]
    rstd = [sbuf(f"n_rstd{h}", [P, 2], f32) for h in range(2)]
    var_set, std_set, passed = sem("n_var_set"), sem("n_std_set"), sem("n_passed")
    up, hid, down, turned, turned_out, lin = (sem(f"n_{n}") for n in ("up", "hid", "down", "turned", "turned_out", "lin"))
    x1_set, h1_set, parts_set, steps = sem("n_x1_set"), sem("n_h1_set"), sem("n_parts_set"), sem("n_steps")
    split = sem("n_split")
    xr_ready = [sem(f"n_xr_ready{h}") for h in range(2)]
    x1_stored, h1_stored, parts_stored = ([sem(f"n_{n}_stored{h}") for h in range(2)] for n in ("x1", "h1", "parts"))

    with nc.Block() as block:
        @block.sync
        def _(sp):
            for h in range(2):
                for k, stored in enumerate((x1_stored, h1_stored, parts_stored)):
                    prime(sp, spare[8 + 3 * h + k:9 + 3 * h + k, :], stored[h], zero)
            with sp.Fori(0, NCH) as c:
                for h in range(2):
                    sp.wait_ge(x1_set, freed(c, h))
                    sp.dma_start(xr[h][:, :, :], x_rows[ds(c * CHUNK + h * NH, NH), :].rearrange("(i p) d -> p i d", p=P)).then_inc(xr_ready[h], 16)
                for h in range(2):
                    sp.wait_ge(x1_set, done(c, h))
                    sp.dma_start(x1_d[ds(c * CHUNK + h * NH, NH), :].rearrange("(i p) d -> p i d", p=P), x1[h][:, :, :]).then_inc(x1_stored[h], 16)
                for h in range(2):
                    sp.wait_ge(h1_set, done(c, h))
                    sp.dma_start(tab0[ds(c * CHUNK + h * NH, NH), :].rearrange("(i p) d -> p i d", p=P), h1[h][:, :, :]).then_inc(h1_stored[h], 16)
                    sp.wait_ge(parts_set, done(c, h))
                    sp.dma_start(h1_parts[ds(c * CHUNK + h * NH, NH), :].rearrange("(i p) d -> p i d", p=P),
                                 parts[h][:, :, :, :].rearrange("p i k d -> p i (k d)")).then_inc(parts_stored[h], 16)
            for h in range(2):
                sp.wait_ge(x1_stored[h], 16 * (NCH + 1))
                sp.wait_ge(h1_stored[h], 16 * (NCH + 1))
                sp.wait_ge(parts_stored[h], 16 * (NCH + 1))

        @block.tensor
        def _(pe):
            for s in (up, down, turned, lin):
                pe.sem_inc(s, CREDIT)
            with pe.Fori(0, NCH) as c:
                for h in range(2):
                    pe.wait_ge(hid, freed(c, h))
                    nc.tensor.matmul(bank[h][:, 0:NH], w_sb["W1"][:, :], aggT[:, ds(c * CHUNK + h * NH, NH)],
                                     start=True, stop=True).then_inc(up, 1)
                for h in range(2):
                    pe.wait_ge(hid, done(c, h))
                    pe.wait_ge(x1_set, freed(c, h))
                    nc.tensor.matmul(bank[2 + h][:, 0:NH], ones3[:, :], bias3["b2"][:, 0:NH], start=True, stop=False)
                    for i in range(2):
                        ins = nc.tensor.matmul(bank[2 + h][:, i * P:i * P + P], hidT[h][:, i * P:i * P + P], w_sb["W2"][:, :],
                                               start=False, stop=(i == 1))
                    ins.then_inc(down, 1)
                for h in range(2):
                    pe.wait_ge(x1_set, done(c, h))
                    pe.wait_ge(turned_out, freed(c, h))
                    for i in range(2):
                        ins = nc.tensor.transpose(bank[4 + h][:, i * P:i * P + P], x1[h][:, i, :], ident[:, :])
                    ins.then_inc(turned, 1)
                for h in range(2):
                    pe.wait_ge(turned_out, done(c, h))
                    pe.wait_ge(h1_set, freed(c, h))
                    for i in range(2):
                        ins = nc.tensor.matmul(bank[6 + h][:, i * P:i * P + P], x1T[h][:, i * P:i * P + P], w_sb["lin1T"][:, :],
                                               start=True, stop=True)
                    ins.then_inc(lin, 1)

        @block.scalar
        def _(act):
            for s in (hid, turned_out, h1_set, std_set):
                act.sem_inc(s, CREDIT)
            with act.Fori(0, NCH) as c:
                for h in range(2):
                    act.wait_ge(up, done(c, h))
                    act.wait_ge(down, freed(c, h))
                    nc.scalar.activation(hidT[h][:, :], bank[h][:, 0:NH], ACT.Relu, bias=b1c[:, 0:1]).then_inc(hid, 1)
                for h in range(2):
                    act.wait_ge(var_set, done(c, h))
                    nc.scalar.activation(std[h][:, :], mean_var[h][:, :, 1], ACT.Sqrt, bias=eps[:, 0:1]).then_inc(std_set, 1)
                for h in range(2):
                    act.wait_ge(turned, done(c, h))
                    act.wait_ge(lin, freed(c, h))
                    nc.scalar.activation(x1T[h][:, :], bank[4 + h][:, 0:NH], ACT.Copy).then_inc(turned_out, 1)
                for h in range(2):
                    act.wait_ge(lin, done(c, h))
                    act.wait_ge(h1_stored[h], 16 * (c + 1))
                    act.wait_ge(parts_set, freed(c, h))
                    nc.scalar.activation(h1[h][:, :, :], bank[6 + h][:, 0:NH].rearrange("p (i d) -> p i d", i=2),
                                         ACT.Copy).then_inc(h1_set, 1)

        @block.vector
        def _(dve):
            for s in (x1_set, parts_set, var_set):
                dve.sem_inc(s, CREDIT)
            with dve.Fori(0, NCH) as c:
                for h in range(2):
                    dve.wait_ge(down, done(c, h))
                    dve.wait_ge(xr_ready[h], 16 * (c + 1))
                    dve.wait_ge(x1_stored[h], 16 * (c + 1))
                    dve.wait_ge(turned, freed(c, h))
                    dve.tensor_tensor(y[h][:, :, :], bank[2 + h][:, 0:NH].rearrange("p (i d) -> p i d", i=2),
                                      xr[h][:, :, :], ALU.add).then_inc(steps, 1)
                    layer_norm_stats(dve, steps, passed, LN_STEPS * c + 5 * h, y[h], stats[h], mean_var[h])
                    dve.wait_ge(steps, LN_STEPS * c + 5 * h + 5)
                    dve.sem_inc(var_set, 1)
                for h in range(2):
                    dve.wait_ge(std_set, done(c, h))
                    layer_norm_apply(dve, steps, passed, LN_STEPS * c + 10 + 3 * h, y[h], mean_var[h], std[h], rstd[h], x1[h])
                    dve.wait_ge(steps, LN_STEPS * c + 13 + 3 * h)
                    dve.sem_inc(x1_set, 1)
                for h in range(2):
                    b = h1[h][:, :, :]
                    at = 8 * c + 4 * h
                    dve.wait_ge(h1_set, done(c, h))
                    dve.wait_ge(parts_stored[h], 16 * (c + 1))
                    dve.tensor_copy(parts[h][:, :, 0, :], b).then_inc(split, 1)
                    dve.wait_ge(split, at + 1)
                    dve.tensor_tensor(rest[h][:, :, 0, :], b, parts[h][:, :, 0, :], ALU.subtract).then_inc(split, 1)
                    dve.wait_ge(split, at + 2)
                    dve.tensor_copy(parts[h][:, :, 2, :], rest[h][:, :, 0, :]).then_inc(split, 1)
                    dve.wait_ge(split, at + 3)
                    dve.tensor_tensor(parts[h][:, :, 1, :], rest[h][:, :, 0, :], parts[h][:, :, 2, :], ALU.subtract).then_inc(split, 1)
                    dve.wait_ge(split, at + 4)
                    dve.sem_inc(parts_set, 1)


def layer1_edge_tables(nc, sem, sbuf, wgt, srcf, repeats, spare_row, scat):
    ALU, ACT = mybir.AluOpType, mybir.ActivationFunctionType
    f32 = mybir.dt.float32
    turns = sbuf("turns", [P, T * SUB], f32)
    u = sbuf("u", [P, T * SUB], f32)
    half_pi = sbuf("half_pi", [P, 1], f32)
    steps, sined = sem("c_steps"), sem("c_sined")
    magic = 1.5 * 2.0 ** 23

    with nc.Block() as block:
        @block.vector
        def _(dve):
            dve.memset(half_pi[:, :], PI / 2).then_inc(steps, 1)
            dve.tensor_scalar(turns[:, :], wgt[:, :], 1.0 / (2 * CUTOFF), magic, ALU.mult, ALU.add).then_inc(steps, 1)
            dve.wait_ge(steps, 2)
            dve.tensor_scalar(turns[:, :], turns[:, :], magic, -2 * CUTOFF, ALU.subtract, ALU.mult).then_inc(steps, 1)
            dve.wait_ge(steps, 3)
            dve.tensor_tensor(u[:, :], wgt[:, :], turns[:, :], ALU.add).then_inc(steps, 1)
            dve.wait_ge(steps, 4)
            dve.scalar_tensor_tensor(u[:, :], u[:, :], -1.0, u[:, :], ALU.mult, ALU.max).then_inc(steps, 1)
            dve.wait_ge(steps, 5)
            dve.tensor_scalar(turns[:, :], srcf[:, :], spare_row[:, 0:1], -1.0, ALU.subtract, ALU.mult).then_inc(steps, 1)
            dve.wait_ge(steps, 6)
            dve.scalar_tensor_tensor(turns[:, :], repeats[:, :], 1.0, turns[:, :], ALU.min, ALU.mult).then_inc(steps, 1)
            dve.wait_ge(steps, 7)
            dve.tensor_tensor(scat[:, :], turns[:, :], srcf[:, :], ALU.add)
            dve.wait_ge(sined, 1)
            dve.tensor_tensor(wgt[:, :], u[:, :], u[:, :], ALU.mult)

        @block.scalar
        def _(act):
            act.wait_ge(steps, 5)
            nc.scalar.activation(u[:, :], u[:, :], ACT.Sin, bias=half_pi[:, 0:1], scale=-PI / (2 * CUTOFF)).then_inc(sined, 1)


def layer1_edges(nc, sem, sbuf, src16, dst16, attr_cols, h1_parts, tabs, srcf, wgt, scat, basef, base, nwin,
                 pidx, spare_row, half, ones3, zero, spare, bias3, nn1, nn2T, bank):
    f32, i32, i16, bf16 = mybir.dt.float32, mybir.dt.int32, mybir.dt.int16, mybir.dt.bfloat16
    ALU, ACT, ds = mybir.AluOpType, mybir.ActivationFunctionType, bass.ds
    attr = [sbuf(f"attr{h}", [1 + GAUSS, HE], f32) for h in range(2)]
    dstb = [sbuf(f"dstb{h}", [P, HE], i16) for h in range(2)]
    srcb = [sbuf(f"srcb1{h}", [P, HE], i16) for h in range(2)]
    h1w = [sbuf(f"h1w{h}", [P, 2 * D], bf16) for h in range(2)]
    soft1 = [sbuf(f"soft1_{h}", [P, HE], f32) for h in range(2)]
    soft2 = [sbuf(f"soft2_{h}", [P, HE], f32) for h in range(2)]
    hid = [sbuf(f"hid{h}", [P, HE], f32) for h in range(2)]
    filt = [sbuf(f"filt{h}", [P, HE], f32) for h in range(2)]
    ohT = [sbuf(f"ohT{h}", [P, HE], bf16) for h in range(2)]
    same = [sbuf(f"same{s}", [P, P], f32) for s in range(SUB)]
    rows = [sbuf(f"rows{h}", [P, HE], f32) for h in range(2)]
    sidx_next = [sbuf(f"sidx_next{h}", [P, HALF], i32) for h in range(2)]
    sidx = [sbuf(f"sidx{h}", [P, HALF], i32) for h in range(2)]
    rel0 = sbuf("rel0", [P, 1], f32)

    attr_in, dstb_in, srcb_in, h1w_in = ([sem(f"{n}_in{h}") for h in range(2)] for n in ("attr", "dstb", "srcb", "h1w"))
    z1_set, z2_set, taken = sem("z1_set"), sem("z2_set"), sem("taken_set")
    exp1, ln1 = sem("exp1"), sem("ln1")
    exp2, ln2 = sem("exp2"), sem("ln2")
    oh_set, same_set, hid_set = sem("oh_set"), sem("same_set"), sem("hid_set")
    filt_set, msg_set = sem("filt_set"), sem("msg_set")
    merged = sem("merged")
    sidx_set, rows_set, stash_set = sem("sidx_set"), sem("rows_set"), sem("stash_set")
    rel_set, zeros_set, z2_zero = sem("rel1_set"), sem("zeros_set"), sem("z2_zero")
    scattered = [sem(f"scattered{s}") for s in range(SUB)]
    passed, passed_sp, passed_dve = sem("e_passed_pool"), sem("e_passed_sp"), sem("e_passed_dve")

    with nc.Block() as block:
        @block.sync
        def _(sp):
            jobs = TileTable(sp, "sp1", nwin, base)
            with sp.Fori(0, T) as t:
                windows = jobs.windows()
                with sp.Fori(0, windows):
                    j = jobs.number()
                    node = jobs.first_node()
                    for h in range(2):
                        wait_apart(sp, z1_set, freed(j, h), passed_sp)
                        sp.dma_start(attr[h][:, :], attr_cols[:, ds(t * TE + h * HE, HE)]).then_inc(attr_in[h], 16)
                        wait_apart(sp, oh_set, freed(j, h), passed_sp)
                        sp.dma_start(dstb[h][:, :], dst16[ds(t, 1), h * HE:(h + 1) * HE].broadcast_to([P, HE])).then_inc(dstb_in[h], 16)
                        wait_apart(sp, same_set, freed(j, h), passed_sp)
                        sp.dma_start(srcb[h][:, :], src16[ds(t, 1), h * HE:(h + 1) * HE].broadcast_to([P, HE])).then_inc(srcb_in[h], 16)
                        wait_apart(sp, taken, freed(j, h), passed_sp)
                        sp.dma_start(h1w[h][0:WIN, :], h1_parts[ds(node, WIN), 0:2 * D]).then_inc(h1w_in[h], 16)
                        sp.dma_start(h1w[h][WIN:P, 0:D], h1_parts[ds(node, WIN), 2 * D:3 * D]).then_inc(h1w_in[h], 16)
                    jobs.read_ahead(t)
                    jobs.step()

        @block.tensor
        def _(pe):
            def first_layer(j, h):
                pe.wait_ge(attr_in[h], 16 * (j + 1))
                pe.wait_ge(hid_set, freed(j, h))
                nc.tensor.matmul(bank[h][:, :], nn1[:, :], attr[h][:, :], start=True, stop=True).then_inc(z1_set, 1)

            def take_h1(j, h):
                pe.wait_ge(oh_set, done(j, h))
                pe.wait_ge(h1w_in[h], 32 * (j + 1))
                pe.wait_ge(msg_set, freed(j, h))
                for s in range(HALF):
                    nc.tensor.matmul(bank[4 + h][:, s * P:s * P + P], ohT[h][:, s * P:s * P + P],
                                     h1w[h][:, 0:D], start=True, stop=False)
                    ins = nc.tensor.matmul(bank[4 + h][:, s * P:s * P + P], ohT[h][0:WIN, s * P:s * P + P],
                                           h1w[h][0:WIN, D:2 * D], start=False, stop=True)
                ins.then_inc(taken, 1)

            def second_layer(j, h):
                pe.wait_ge(filt_set, freed(j, h))
                nc.tensor.matmul(bank[2 + h][:, :], ones3[:, :], bias3["nnb2"][:, :], start=True, stop=False)
                pe.wait_ge(hid_set, done(j, h))
                for s in range(HALF):
                    ins = nc.tensor.matmul(bank[2 + h][:, s * P:s * P + P], hid[h][:, s * P:s * P + P], nn2T[:, :],
                                           start=False, stop=(s == HALF - 1))
                ins.then_inc(z2_set, 1)

            def merge_before(j, h):
                pe.wait_ge(msg_set, freed(j, h))
                pe.wait_ge(rows_set, freed(j - 1, h))
                for s in range(HALF):
                    ins = nc.tensor.matmul(bank[6 + h][:, s * P:s * P + P], same[h * HALF + s][:, :],
                                           filt[h][:, s * P:s * P + P], start=True, stop=True)
                ins.then_inc(merged, 1)

            for s in (z1_set, z2_set, taken):
                pe.sem_inc(s, CREDIT)
            pe.sem_inc(merged, CREDIT - 2)
            pe.wait_ge(zeros_set, SUB + 1)
            nc.tensor.matmul(bank[3][:, :], ones3[:, :], bias3["nnb2"][:, :], start=True, stop=True)
            nc.tensor.matmul(bank[5][:, :], ones3[:, :], bias3["nnb2"][:, :], start=True, stop=True).then_inc(z2_zero, 1)
            jobs = TileTable(pe, "pe1", nwin)
            with pe.Fori(0, T) as t:
                windows = jobs.windows()
                with pe.Fori(0, windows):
                    j = jobs.number()
                    first_layer(j, 0)
                    merge_before(j, 0)
                    first_layer(j, 1)
                    take_h1(j, 0)
                    jobs.read_ahead(t)
                    second_layer(j, 0)
                    merge_before(j, 1)
                    take_h1(j, 1)
                    second_layer(j, 1)
                    jobs.step()
            end = jobs.number()
            merge_before(end, 0)
            merge_before(end, 1)

        @block.scalar
        def _(act):
            def soften(j, h, z, buf, made, used, s_exp, s_ln):
                act.wait_ge(made, done(j, h))
                act.wait_ge(used, freed(j, h))
                nc.scalar.activation(buf[:, :], z[:, :], ACT.Exp).then_inc(s_exp, 1)
                act.wait_ge(s_exp, done(j, h))
                nc.scalar.activation(buf[:, :], buf[:, :], ACT.Ln, bias=half[:, 0:1]).then_inc(s_ln, 1)

            def soften1(j, h):
                soften(j, h, bank[h], soft1[h], z1_set, hid_set, exp1, ln1)

            def soften2(j, h):
                soften(j, h, bank[2 + h], soft2[h], z2_set, filt_set, exp2, ln2)

            def rows_before(j, h):
                for s in range(HALF):
                    act.wait_ge(scattered[h * HALF + s], 16 * (j + 1))
                act.wait_ge(stash_set, freed(j, h))
                nc.scalar.activation(sidx[h][:, :], sidx_next[h][:, :], ACT.Copy).then_inc(sidx_set, 1)
                act.wait_ge(merged, freed(j, h))
                nc.scalar.activation(rows[h][:, :], bank[6 + h][:, :], ACT.Copy).then_inc(rows_set, 1)

            def stash_rows(j, h, here):
                act.wait_ge(sidx_set, freed(j, h))
                nc.scalar.activation(sidx_next[h][:, :], scat[:, ds(here + h * HALF, HALF)], ACT.Copy).then_inc(stash_set, 1)

            nc.scalar.preload_act_table_set("natural_log_exp_and_others")
            for s in (exp1, ln1):
                act.sem_inc(s, CREDIT)
            for s in (exp2, ln2):
                act.sem_inc(s, CREDIT - 1)
            for s in (rows_set, sidx_set, stash_set):
                act.sem_inc(s, CREDIT - 2)
            for h in range(2):
                nc.scalar.activation(sidx_next[h][:, :], spare_row[:, 0:1].broadcast_to([P, HALF]), ACT.Copy).then_inc(stash_set, 1)
            act.wait_ge(z2_zero, 1)
            jobs = TileTable(act, "act1", nwin)
            with act.Fori(0, T) as t:
                windows = jobs.windows()
                here = act.snap(t * SUB, min_val=0, max_val=(T - 1) * SUB)
                with act.Fori(0, windows):
                    j = jobs.number()
                    soften1(j, 0)
                    soften2(j - 1, 1)
                    rows_before(j, 0)
                    stash_rows(j, 0, here)
                    soften1(j, 1)
                    jobs.read_ahead(t)
                    soften2(j, 0)
                    rows_before(j, 1)
                    stash_rows(j, 1, here)
                    jobs.step()
            end = jobs.number()
            soften2(end - 1, 1)
            rows_before(end, 0)
            rows_before(end, 1)

        @block.gpsimd
        def _(pool):
            def scatter_before(j, h):
                pool.wait_ge(sidx_set, freed(j, h))
                for s in range(HALF):
                    g = h * HALF + s
                    pool.wait_ge(scattered[g], 16 * (j + 1))
                    if s == 0:
                        wait_apart(pool, rows_set, freed(j, h), passed)
                    else:
                        pool.sem_inc(passed, 1)
                    pool.indirect_dma_start(tabs[g], bass.IndirectOffsetOnAxis(ap=sidx[h][:, s:s + 1], axis=0),
                                            rows[h][:, s * P:s * P + P], None, compute_op=ALU.add).then_inc(scattered[g], 16)

            for g in range(SUB):
                prime(pool, spare[16 + g:17 + g, :], scattered[g], zero)
            jobs = TileTable(pool, "pool1", nwin)
            with pool.Fori(0, T) as t:
                windows = jobs.windows()
                with pool.Fori(0, windows):
                    j = jobs.number()
                    scatter_before(j, 0)
                    jobs.read_ahead(t)
                    scatter_before(j, 1)
                    jobs.step()
            end = jobs.number()
            scatter_before(end, 0)
            scatter_before(end, 1)
            for g in range(SUB):
                pool.wait_ge(scattered[g], 16 * (end + 2))

        @block.vector
        def _(dve):
            def one_hot(j, h):
                dve.wait_ge(dstb_in[h], 16 * (j + 1))
                dve.wait_ge(taken, freed(j, h))
                dve.tensor_single_scalar(ohT[h][:, :], dstb[h][:, :], rel0[:, 0:1], ALU.is_equal).then_inc(oh_set, 1)

            def equal_src(j, h, here):
                dve.wait_ge(srcb_in[h], 16 * (j + 1))
                dve.wait_ge(merged, freed(j, h))
                for s in range(HALF):
                    at = ds(here + h * HALF + s, 1)
                    ins = dve.tensor_scalar(same[h * HALF + s][:, :], srcb[h][:, s * P:s * P + P], srcf[:, at], wgt[:, at],
                                            ALU.is_equal, ALU.mult)
                ins.then_inc(same_set, 1)

            def hidden(j, h):
                dve.wait_ge(ln1, done(j, h))
                dve.wait_ge(z2_set, freed(j, h))
                dve.scalar_tensor_tensor(hid[h][:, :], soft1[h][:, :], SURE, bank[h][:, :], ALU.min, ALU.max).then_inc(hid_set, 1)

            def message(j, h, merges):
                dve.wait_ge(ln2, done(j, h))
                dve.wait_ge(merged, merges)
                dve.scalar_tensor_tensor(filt[h][:, :], soft2[h][:, :], SURE, bank[2 + h][:, :], ALU.min, ALU.max).then_inc(filt_set, 1)
                dve.wait_ge(taken, done(j, h))
                dve.wait_ge(filt_set, done(j, h))
                dve.tensor_tensor(filt[h][:, :], filt[h][:, :], bank[4 + h][:, :], ALU.mult).then_inc(msg_set, 1)

            for s in (oh_set, same_set, hid_set):
                dve.sem_inc(s, CREDIT)
            for s in (filt_set, msg_set):
                dve.sem_inc(s, CREDIT - 1)
            dve.sem_inc(rel_set, 1)
            dve.memset(filt[0][:, :], 0.0).then_inc(zeros_set, 1)
            for s in range(SUB):
                dve.memset(same[s][:, :], 0.0).then_inc(zeros_set, 1)
            jobs = TileTable(dve, "dve1", nwin)
            with dve.Fori(0, T) as t:
                windows = jobs.windows()
                j0 = jobs.number()
                here = dve.snap(t * SUB, min_val=0, max_val=(T - 1) * SUB)
                dve.wait_ge(rel_set, t + j0 + 1)
                dve.tensor_tensor(rel0[:, :], pidx[:, :], basef[:, ds(t, 1)], ALU.add).then_inc(rel_set, 1)
                with dve.Fori(0, windows):
                    j = jobs.number()
                    hidden(j, 0)
                    dve.wait_ge(rel_set, t + j + 2)
                    one_hot(j, 0)
                    one_hot(j, 1)
                    message(j - 1, 1, freed(j - 1, 1))
                    equal_src(j, 0, here)
                    hidden(j, 1)
                    jobs.read_ahead(t)
                    dve.wait_ge(oh_set, done(j, 1))
                    dve.tensor_single_scalar(rel0[:, :], rel0[:, :], float(WIN), ALU.add).then_inc(rel_set, 1)
                    equal_src(j, 1, here)
                    message(j, 0, freed(j, 0))
                    jobs.step()
            message(jobs.number() - 1, 1, freed(jobs.number() - 1, 1))


def layer1_nodes(nc, sem, sbuf, x1_d, tabs, lin2T, bias3, ones3, ident, eps, zero, spare, bank, out):
    f32 = mybir.dt.float32
    ALU, ACT, ds = mybir.AluOpType, mybir.ActivationFunctionType, bass.ds
    tab = [[sbuf(f"tab{h}_{k}", [P, 2, D], f32) for k in range(NTAB)] for h in range(2)]
    h2T = [sbuf(f"f_h2T{h}", [P, NH], f32) for h in range(2)]
    x1 = [sbuf(f"f_x1{h}", [P, 2, D], f32) for h in range(2)]
    y = [sbuf(f"f_y{h}", [P, 2, D], f32) for h in range(2)]
    o = [sbuf(f"f_o{h}", [P, 2, D], f32) for h in range(2)]
    stats = [sbuf(f"f_stats{h}", [P, 2, 6], f32) for h in range(2)]
    mean_var = [sbuf(f"f_mv{h}", [P, 2, 2], f32) for h in range(2)]
    std = [sbuf(f"f_std{h}", [P, 2], f32) for h in range(2)]
    rstd = [sbuf(f"f_rstd{h}", [P, 2], f32) for h in range(2)]
    var_set, std_set, passed = sem("f_var_set"), sem("f_std_set"), sem("f_passed")
    loaded = [sem(f"f_loaded{h}") for h in range(2)]
    stored = [sem(f"f_stored{h}") for h in range(2)]
    turned, turned_out, lin, steps, o_set = (sem(f"f_{n}") for n in ("turned", "turned_out", "lin", "steps", "o_set"))
    nload = 16 * (NTAB + 1)

    with nc.Block() as block:
        @block.sync
        def _(sp):
            with sp.Fori(0, NCH) as c:
                for h in range(2):
                    at = ds(c * CHUNK + h * NH, NH)
                    sp.wait_ge(turned, freed(c, h))
                    sp.wait_ge(o_set, freed(c, h))
                    for k in range(NTAB):
                        sp.dma_start(tab[h][k][:, :, :], tabs[k][at, :].rearrange("(i p) d -> p i d", p=P)).then_inc(loaded[h], 16)
                    sp.dma_start(x1[h][:, :, :], x1_d[at, :].rearrange("(i p) d -> p i d", p=P)).then_inc(loaded[h], 16)

        @block.tensor
        def _(pe):
            for s in (turned, lin):
                pe.sem_inc(s, CREDIT)
            with pe.Fori(0, NCH) as c:
                for h in range(2):
                    pe.wait_ge(loaded[h], nload * (c + 1))
                    pe.wait_ge(turned_out, freed(c, h))
                    for i in range(2):
                        for k in range(NTAB):
                            ins = nc.tensor.matmul(bank[h][:, i * P:i * P + P], tab[h][k][:, i, :], ident[:, :],
                                                   start=(k == 0), stop=(k == NTAB - 1))
                    ins.then_inc(turned, 1)
                for h in range(2):
                    pe.wait_ge(turned_out, done(c, h))
                    pe.wait_ge(o_set, freed(c, h))
                    nc.tensor.matmul(bank[2 + h][:, 0:NH], ones3[:, :], bias3["lin2b"][:, 0:NH], start=True, stop=False)
                    for i in range(2):
                        ins = nc.tensor.matmul(bank[2 + h][:, i * P:i * P + P], h2T[h][:, i * P:i * P + P], lin2T[:, :],
                                               start=False, stop=(i == 1))
                    ins.then_inc(lin, 1)

        @block.scalar
        def _(act):
            act.sem_inc(turned_out, CREDIT)
            act.sem_inc(std_set, CREDIT)
            for h in range(2):
                prime(act, spare[24 + h:25 + h, :], stored[h], zero)
            with act.Fori(0, NCH) as c:
                for h in range(2):
                    act.wait_ge(turned, done(c, h))
                    act.wait_ge(lin, freed(c, h))
                    nc.scalar.activation(h2T[h][:, :], bank[h][:, 0:NH], ACT.Copy).then_inc(turned_out, 1)
                for h in range(2):
                    act.wait_ge(var_set, done(c, h))
                    nc.scalar.activation(std[h][:, :], mean_var[h][:, :, 1], ACT.Sqrt, bias=eps[:, 0:1]).then_inc(std_set, 1)
                for h in range(2):
                    act.wait_ge(o_set, done(c, h))
                    act.dma_start(out[ds(c * CHUNK + h * NH, NH), :].rearrange("(i p) d -> p i d", p=P), o[h][:, :, :]).then_inc(stored[h], 16)
            for h in range(2):
                act.wait_ge(stored[h], 16 * (NCH + 1))

        @block.vector
        def _(dve):
            dve.sem_inc(o_set, CREDIT)
            dve.sem_inc(var_set, CREDIT)
            with dve.Fori(0, NCH) as c:
                for h in range(2):
                    dve.wait_ge(lin, done(c, h))
                    dve.wait_ge(loaded[h], nload * (c + 1))
                    dve.wait_ge(stored[h], 16 * (c + 1))
                    dve.tensor_tensor(y[h][:, :, :], bank[2 + h][:, 0:NH].rearrange("p (i d) -> p i d", i=2),
                                      x1[h][:, :, :], ALU.add).then_inc(steps, 1)
                    layer_norm_stats(dve, steps, passed, LN_STEPS * c + 5 * h, y[h], stats[h], mean_var[h])
                    dve.wait_ge(steps, LN_STEPS * c + 5 * h + 5)
                    dve.sem_inc(var_set, 1)
                for h in range(2):
                    dve.wait_ge(std_set, done(c, h))
                    layer_norm_apply(dve, steps, passed, LN_STEPS * c + 10 + 3 * h, y[h], mean_var[h], std[h], rstd[h], o[h])
                    dve.wait_ge(steps, LN_STEPS * c + 13 + 3 * h)
                    dve.sem_inc(o_set, 1)


_OUTS = [((NPAD, D), "float32")]


def kernel(x, src, dst, edge_attr_50, edge_weight, L0_gnn_W1, L0_gnn_b1, L0_gnn_W2, L0_gnn_b2,
           L1_gnn_lin1_w, L1_gnn_nn_w1, L1_gnn_nn_b1, L1_gnn_nn_w2, L1_gnn_nn_b2, L1_gnn_lin2_w, L1_gnn_lin2_b):
    import numpy as np
    import concourse.bacc as bacc
    from concourse.bass_utils import run_bass_kernel_spmd

    x, src, dst, attr, w = (np.asarray(a) for a in (x, src, dst, edge_attr_50, edge_weight))
    pad = EPAD - E
    src = np.concatenate([src, np.arange(N, N + pad, dtype=src.dtype)])
    dst = np.concatenate([dst, np.full(pad, N - 1, dst.dtype)])
    w = np.concatenate([w, np.zeros(pad, w.dtype)])
    xp = np.zeros((NPAD, D), x.dtype)
    xp[:N] = x
    at = np.zeros((1 + GAUSS, EPAD), attr.dtype)
    at[0] = 1
    at[1:, :E] = attr.T

    def cols(a):
        return np.ascontiguousarray(a.reshape(T * SUB, P).T)

    row = lambda a: np.asarray(a).reshape(1, D)
    tr = lambda a: np.ascontiguousarray(np.asarray(a).T)
    ins = {
        "x_rows": xp, "x_cols": tr(xp), "src_cols": cols(src), "dst_cols": cols(dst), "w_cols": cols(w),
        "src_rows": src.reshape(T, TE), "dst_rows": dst.reshape(T, TE), "attr_cols": at,
        "W1": np.asarray(L0_gnn_W1), "b1": np.asarray(L0_gnn_b1).reshape(D, 1), "W2": np.asarray(L0_gnn_W2),
        "b2": row(L0_gnn_b2), "lin1T": tr(L1_gnn_lin1_w),
        "nn1T": np.concatenate([row(L1_gnn_nn_b1), tr(L1_gnn_nn_w1)]), "nn2T": tr(L1_gnn_nn_w2),
        "nnb2": row(L1_gnn_nn_b2), "lin2T": tr(L1_gnn_lin2_w), "lin2b": row(L1_gnn_lin2_b),
    }
    nc = bacc.Bacc("TRN2", target_bir_lowering=False, num_devices=1)
    args = {n: nc.dram_tensor(n, a.shape, mybir.dt.from_np(a.dtype), kind="ExternalInput").ap() for n, a in ins.items()}
    out = nc.dram_tensor("out", (NPAD, D), mybir.dt.float32, kind="ExternalOutput").ap()
    edge_network_kernel(nc, out=out, **args)
    r = run_bass_kernel_spmd(nc, [ins], core_ids=[0])
    return r.results[0]["out"][:N]
```

```python
from contextlib import ExitStack

import concourse.bass as bass
from concourse import mybir

D = 128
P = 128
N = 12500
E = 412500
GAUSS = 50
UNIT = 512
G = UNIT // P
UNITS = -(-N // UNIT)
NPAD = UNITS * UNIT
SUB = 8
HALF = SUB // 2
HE = HALF * P
TE = SUB * P
T = -(-E // TE)
EPAD = T * TE
NGRP = -(-T // P)
WIN = 64
SPARE = NPAD
ZROWS = -(-(NPAD + P) // T)
TROWS = T * ZROWS
NTAB = HALF
MAXJOBS = T * (-(-N // WIN))
LN_EPS = 1e-5
CREDIT = 4
CUTOFF = 10.0
PI = 3.141592653589793


def edge_network_kernel(nc, x_rows, x_cols, src_cols, dst_cols, w_cols, src_rows, dst_rows,
                        attr_cols, W1, b1, W2, b2, lin1T, nn1T, nn2T, nnb2, lin2T, lin2b, out):
    f32, i32, i16, bf16 = mybir.dt.float32, mybir.dt.int32, mybir.dt.int16, mybir.dt.bfloat16
    ALU = mybir.AluOpType
    ACT = mybir.ActivationFunctionType
    AX = mybir.AxisListType
    ds = bass.ds

    ctx = ExitStack()
    with ctx:
        def sb(name, shape, dt):
            return ctx.enter_context(nc.sbuf_tensor(name, shape, dt))

        def sem(name):
            return ctx.enter_context(nc.semaphore(name))

        src16 = nc.dram_tensor("src16", [T, TE], i16, kind="Internal").ap()
        dst16 = nc.dram_tensor("dst16", [T, TE], i16, kind="Internal").ap()
        base_d = nc.dram_tensor("base_d", [NGRP * P, 1], i32, kind="Internal").ap()
        nwin_d = nc.dram_tensor("nwin_d", [NGRP * P, 1], i32, kind="Internal").ap()
        x1_d = nc.dram_tensor("x1_d", [NPAD, D], f32, kind="Internal").ap()
        h1_parts = nc.dram_tensor("h1_parts", [NPAD, 3 * D], bf16, kind="Internal").ap()
        spare = nc.dram_tensor("spare", [32, 16], f32, kind="Internal").ap()
        tabs = [nc.dram_tensor(f"sum_table{k}", [TROWS, D], f32, kind="Internal").ap()
                for k in range(NTAB)]

        srcf = sb("srcf", [P, T * SUB], f32)
        dstf = sb("dstf", [P, T * SUB], f32)
        wgt = sb("wgt", [P, T * SUB], f32)
        repeats = sb("repeats", [P, T * SUB], f32)
        scat = sb("scat", [P, T * SUB], i32)
        base = sb("base", [P, T + 1], i32)
        basef = sb("basef", [P, T], f32)
        nwin = sb("nwin", [P, T + 1], i32)
        ident = sb("ident", [P, P], f32)
        tri = sb("tri", [P, P], f32)
        cols = sb("cols", [P, WIN], f32)
        pidx = sb("pidx", [P, 1], f32)
        spare_row = sb("spare_row", [P, 1], f32)
        eps = sb("eps", [P, 1], f32)
        ones3 = sb("ones3", [3, P], bf16)
        bias3 = {n: sb(f"bias3_{n}", [3, HE], bf16) for n in ("b2", "nnb2", "lin2b")}
        zero = sb("zero", [P, D], f32)
        w_sb = {n: sb(f"w_{n}", [P, D], f32) for n in ("W1", "W2", "lin1T", "nn2T", "lin2T")}
        nn1 = sb("nn1", [GAUSS + 1, D], f32)
        b1c = sb("b1c", [P, 1], f32)
        bank = [ctx.enter_context(nc.psum_tensor(f"bank{i}", [P, 512], f32)) for i in range(8)]

        layer0 = ctx.enter_context(ExitStack())
        aggT = layer0.enter_context(nc.sbuf_tensor("aggT", [D, NPAD], f32))
        x_loaded = sem("x_loaded")
        gathered = [sem(f"gathered{s}") for s in range(SUB)]
        scattered = [sem(f"scattered{s}") for s in range(NTAB)]

        with ExitStack() as c0:
            def sb0(name, shape, dt):
                return c0.enter_context(nc.sbuf_tensor(name, shape, dt))

            rows_i = sb0("rows_i", [P, NGRP, 2, TE], i32)
            rows_h = sb0("rows_h", [P, NGRP, 2, TE], i16)
            least = sb0("least", [P, NGRP], i32)
            most = sb0("most", [P, NGRP], i32)
            brow = sb0("brow", [1, 3, D], f32)
            bpart = sb0("bpart", [1, 3, 3, 4, D], bf16)
            brest = sb0("brest", [1, 2, 3, D], f32)
            dst_in, src_in = ([sem(f"{n}_rows_in{i}") for i in range(NGRP)] for n in ("dst", "src"))
            src_cols_in, dst_cols_in, w_in = sem("src_cols_in"), sem("dst_cols_in"), sem("w_in")
            s_brow, s_pool, s_win, s_split = sem("bias_rows"), sem("pool_consts"), sem("windows"), sem("split_step")
            dst_half, src_half = sem("dst_halved"), sem("src_halved")
            win_st, nn1_in, s_st, s_tab, s_b3 = sem("windows_stored"), sem("nn1_in"), sem("scratch_stored"), sem("table_loaded"), sem("bias_moved")
            s_fin, s_dv = sem("setup_cols"), sem("window_steps")
            g = [min(P, T - P * i) for i in range(NGRP)]

            with nc.Block() as block:
                @block.sync
                def _(sp):
                    for i in range(NGRP):
                        sp.dma_start(rows_i[0:g[i], i, 0, :], dst_rows[P * i:P * i + g[i], :]).then_inc(dst_in[i], 16)
                    for i in range(NGRP):
                        sp.dma_start(rows_i[0:g[i], i, 1, :], src_rows[P * i:P * i + g[i], :]).then_inc(src_in[i], 16)
                    sp.wait_ge(s_win, 1)
                    for i in range(NGRP):
                        sp.dma_start(base_d[P * i:P * i + g[i], :], least[0:g[i], i:i + 1]).then_inc(win_st, 16)
                        sp.dma_start(nwin_d[P * i:P * i + g[i], :], most[0:g[i], i:i + 1]).then_inc(win_st, 16)
                    for i in range(NGRP):
                        sp.wait_ge(dst_half, i + 1)
                        sp.dma_start(dst16[P * i:P * i + g[i], :], rows_h[0:g[i], i, 0, :]).then_inc(s_st, 16)
                        sp.wait_ge(src_half, i + 1)
                        sp.dma_start(src16[P * i:P * i + g[i], :], rows_h[0:g[i], i, 1, :]).then_inc(s_st, 16)
                    sp.wait_ge(win_st, 16 * 2 * NGRP)
                    sp.dma_start(base[:, 0:T], base_d[0:T, :].rearrange("t o -> o t").broadcast_to([P, T])).then_inc(s_tab, 16)
                    sp.dma_start(nwin[:, 0:T], nwin_d[0:T, :].rearrange("t o -> o t").broadcast_to([P, T])).then_inc(s_tab, 16)
                    sp.wait_ge(s_split, 5)
                    for i, n in enumerate(("b2", "nnb2", "lin2b")):
                        for k in range(3):
                            sp.dma_start(bias3[n][k:k + 1, :], bpart[0:1, k, i, :, :].rearrange("o a d -> o (a d)")).then_inc(s_b3, 16)
                    sp.wait_ge(s_st, 16 * 2 * NGRP)
                    sp.wait_ge(s_b3, 16 * 9)
                    sp.wait_ge(s_tab, 32)

                @block.scalar
                def _(act):
                    for i, v in enumerate((b2, nnb2, lin2b)):
                        act.dma_start(brow[0:1, i, :], v).then_inc(s_brow, 16)
                    act.dma_start(nn1[:, :], nn1T).then_inc(nn1_in, 16)
                    act.dma_start(scat[:, :], src_cols).then_inc(src_cols_in, 16)
                    act.dma_start(wgt[:, :], w_cols).then_inc(w_in, 16)
                    for i in range(NGRP):
                        act.wait_ge(dst_in[i], 16)
                        nc.scalar.activation(rows_h[0:g[i], i, 0, :], rows_i[0:g[i], i, 0, :], ACT.Copy).then_inc(dst_half, 1)
                    act.wait_ge(src_cols_in, 16)
                    nc.scalar.activation(srcf[:, :], scat[:, :], ACT.Copy).then_inc(s_fin, 1)
                    act.wait_ge(s_fin, 1)
                    act.dma_start(scat[:, :], dst_cols).then_inc(dst_cols_in, 16)
                    act.wait_ge(dst_cols_in, 16)
                    nc.scalar.activation(dstf[:, :], scat[:, :], ACT.Copy).then_inc(s_fin, 1)
                    act.wait_ge(w_in, 16)
                    act.wait_ge(nn1_in, 16)

                @block.gpsimd
                def _(pool):
                    pool.memset(zero[:, :], 0.0).then_inc(s_pool, 1)
                    pool.wait_ge(s_pool, 1)
                    for s in range(SUB):
                        prime(pool, spare[s:s + 1, :], gathered[s], zero)
                    pool.memset(ident[:, :], 0.0).then_inc(s_pool, 1)
                    pool.memset(tri[:, :], 1.0).then_inc(s_pool, 1)
                    pool.memset(ones3[:, :], 1.0).then_inc(s_pool, 1)
                    pool.memset(nwin[:, T:T + 1], 1).then_inc(s_pool, 1)
                    pool.memset(base[:, T:T + 1], 0).then_inc(s_pool, 1)
                    pool.memset(eps[:, :], LN_EPS).then_inc(s_pool, 1)
                    pool.iota(cols[:, :], pattern=[[1, WIN]], base=0, channel_multiplier=0,
                              allow_small_or_imprecise_dtypes=True).then_inc(s_pool, 1)
                    pool.iota(pidx[:, :], pattern=[[0, 1]], base=0, channel_multiplier=1,
                              allow_small_or_imprecise_dtypes=True).then_inc(s_pool, 1)
                    pool.iota(spare_row[:, :], pattern=[[0, 1]], base=SPARE, channel_multiplier=1,
                              allow_small_or_imprecise_dtypes=True).then_inc(s_pool, 1)
                    pool.wait_ge(s_pool, 10)
                    pool.affine_select(out=ident[:, :], in_=ident[:, :], compare_op=ALU.not_equal, fill=1.0,
                                       base=0, pattern=[[-1, P]], channel_multiplier=1)
                    pool.affine_select(out=tri[:, :], in_=tri[:, :], compare_op=ALU.is_gt, fill=0.0,
                                       base=0, pattern=[[-1, P]], channel_multiplier=1)
                    for s in range(SUB):
                        pool.wait_ge(gathered[s], 16)

                @block.vector
                def _(dve):
                    for i in range(NGRP):
                        dve.wait_ge(dst_in[i], 16)
                        dve.tensor_reduce(least[0:g[i], i:i + 1], rows_i[0:g[i], i, 0, :], axis=AX.X, op=ALU.min).then_inc(s_dv, 1)
                        dve.tensor_reduce(most[0:g[i], i:i + 1], rows_i[0:g[i], i, 0, :], axis=AX.X, op=ALU.max).then_inc(s_dv, 1)
                    at = 2 * NGRP
                    for op in (lambda a, b: dve.tensor_tensor(a, a, b, ALU.subtract),
                               lambda a, b: dve.tensor_single_scalar(a, a, 6, ALU.arith_shift_right),
                               lambda a, b: dve.tensor_single_scalar(a, a, 1, ALU.add)):
                        dve.wait_ge(s_dv, at)
                        for i in range(NGRP):
                            op(most[0:g[i], i:i + 1], least[0:g[i], i:i + 1]).then_inc(s_dv, 1)
                        at += NGRP
                    dve.wait_ge(s_dv, at)
                    dve.sem_inc(s_win, 1)
                    for i in range(NGRP):
                        dve.wait_ge(src_in[i], 16)
                        dve.tensor_copy(rows_h[0:g[i], i, 1, :], rows_i[0:g[i], i, 1, :]).then_inc(src_half, 1)
                    dve.wait_ge(s_brow, 48)
                    hi, mid, lo = (bpart[0:1, k, :, 0, :] for k in range(3))
                    dve.tensor_copy(hi, brow[:, :, :]).then_inc(s_split, 1)
                    dve.wait_ge(s_split, 1)
                    dve.tensor_tensor(brest[:, 0, :, :], brow[:, :, :], hi, ALU.subtract).then_inc(s_split, 1)
                    dve.wait_ge(s_split, 2)
                    dve.tensor_copy(mid, brest[:, 0, :, :]).then_inc(s_split, 1)
                    dve.wait_ge(s_split, 3)
                    dve.tensor_tensor(lo, brest[:, 0, :, :], mid, ALU.subtract).then_inc(s_split, 1)
                    dve.wait_ge(s_split, 4)
                    dve.tensor_copy(bpart[:, :, :, 1:4, :].rearrange("o k i a d -> o (k i) a d"),
                                    bpart[:, :, :, 0:1, :].rearrange("o k i a d -> o (k i) a d")
                                    .broadcast_to([1, 9, 3, D])).then_inc(s_split, 1)
                    dve.wait_ge(s_tab, 32)
                    dve.tensor_copy(basef[:, :], base[:, 0:T])
                    dve.wait_ge(s_pool, 10)
                    dve.tensor_single_scalar(pidx[WIN:P, :], pidx[WIN:P, :], float(WIN), ALU.subtract)

        with ExitStack() as c1:
            def sb1(name, shape, dt):
                return c1.enter_context(nc.sbuf_tensor(name, shape, dt))

            with ExitStack() as c2:
                def sb2(name, shape, dt):
                    return c2.enter_context(nc.sbuf_tensor(name, shape, dt))

                gidx = [sb2(f"gidx{h}", [P, HALF], i32) for h in range(2)]
                xg = [sb2(f"xg{s}", [P, D], f32) for s in range(SUB)]
                onehot = [sb2(f"onehot{h}", [P, HALF, WIN], f32) for h in range(2)]
                srcb = [sb2(f"srcb{h}", [P, HE], i16) for h in range(2)]
                eq = [sb2(f"eq{s}", [P, P], bf16) for s in range(SUB)]
                dup = sb2("dup", [P, SUB], f32)
                rel = sb2("rel", [P, SUB], f32)
                tables_zero, weights_in = sem("tables_zero"), sem("weights_in")
                gidx_ready = [sem(f"gidx_ready{h}") for h in range(2)]
                summed = sem("summed")
                onehot_ready = sem("onehot_ready")
                srcb_ready = [sem(f"srcb_ready{h}") for h in range(2)]
                dups_done = sem("dups_done")
                flushed = sem("flushed")
                rel_set = sem("rel_set")
                passed, scat_set, hot_set = sem("passed_pool"), sem("repeats_kept"), sem("hot_set")

                with nc.Block() as block:
                    @block.sync
                    def _(sp):
                        sp.dma_start(aggT[:, :], x_cols).then_inc(x_loaded, 16)
                        for n, v in (("W1", W1), ("W2", W2), ("lin1T", lin1T), ("nn2T", nn2T), ("lin2T", lin2T)):
                            sp.dma_start(w_sb[n][:, :], v).then_inc(weights_in, 16)
                        sp.dma_start(b1c[:, :], b1).then_inc(weights_in, 16)
                        jobs = TileTable(sp, "sp0", nwin)
                        with sp.Fori(0, T) as t:
                            windows = jobs.windows()
                            with sp.Fori(0, windows):
                                j = jobs.number()
                                jobs.read_ahead(t)
                                for h in range(2):
                                    sp.wait_ge(dups_done, freed(j, h))
                                    sp.dma_start(srcb[h][:, :], src16[ds(t, 1), h * HE:(h + 1) * HE]
                                                 .broadcast_to([P, HE])).then_inc(srcb_ready[h], 16)
                                jobs.step()
                        sp.wait_ge(weights_in, 16 * 6)

                    @block.scalar
                    def _(act):
                        act.dma_start(tabs[0][NPAD:NPAD + P, :], zero[:, 0:D]).then_inc(tables_zero, 16)
                        jobs = TileTable(act, "act0", nwin)
                        with act.Fori(0, T) as t:
                            windows = jobs.windows()
                            for k in range(1, NTAB):
                                act.dma_start(tabs[k][ds(t * ZROWS, ZROWS), :], zero[0:ZROWS, 0:D]).then_inc(tables_zero, 16)
                            with act.Fori(0, windows):
                                j = jobs.number()
                                jobs.read_ahead(t)
                                for h in range(2):
                                    for s in range(HALF * h, HALF * h + HALF):
                                        act.wait_ge(gathered[s], 16 * (j + 1))
                                    nc.scalar.activation(gidx[h][:, :], srcf[:, ds(t * SUB + HALF * h, HALF)],
                                                         ACT.Copy).then_inc(gidx_ready[h], 1)
                                jobs.step()
                        act.wait_ge(tables_zero, 16 * (1 + (NTAB - 1) * T))

                    @block.gpsimd
                    def _(pool):
                        jobs = TileTable(pool, "pool0", nwin)
                        with pool.Fori(0, T) as t:
                            windows = jobs.windows()
                            with pool.Fori(0, windows):
                                j = jobs.number()
                                for s in range(SUB):
                                    if s == HALF + 1:
                                        jobs.read_ahead(t)
                                    if s % HALF == 0:
                                        pool.wait_ge(gidx_ready[s // HALF], j + 1)
                                    wait_apart(pool, summed, SUB * j + s + 1, passed)
                                    pool.indirect_dma_start(
                                        xg[s][:, :], None, x_rows,
                                        bass.IndirectOffsetOnAxis(ap=gidx[s // HALF][:, s % HALF:s % HALF + 1], axis=0),
                                    ).then_inc(gathered[s], 16)
                                jobs.step()

                    @block.tensor
                    def _(pe):
                        pe.sem_inc(summed, SUB)
                        jobs = TileTable(pe, "pe0", nwin)
                        with pe.Fori(0, T) as t:
                            windows = jobs.windows()
                            with pe.Fori(0, windows):
                                j = jobs.number()
                                for s in range(SUB):
                                    h = s // HALF
                                    if s == HALF:
                                        jobs.read_ahead(t)
                                    if s % HALF == 0:
                                        pe.wait_ge(flushed, freed(j, h))
                                    pe.wait_ge(gathered[s], 16 * (j + 2))
                                    if s % HALF == 0:
                                        pe.wait_ge(onehot_ready, 2 * j + h + 1)
                                    nc.tensor.matmul(bank[h][:, 0:WIN], xg[s][:, :], onehot[h][:, s % HALF, :],
                                                     start=(s % HALF == 0), stop=(s % HALF == HALF - 1)).then_inc(summed, 1)
                                jobs.step()

                    @block.vector
                    def _(dve):
                        dve.sem_inc(dups_done, CREDIT)
                        dve.sem_inc(flushed, CREDIT)
                        dve.sem_inc(scat_set, 1)
                        cols3 = cols[:, :].rearrange("p (o w) -> p o w", o=1)
                        jobs = TileTable(dve, "dve0", nwin, base)
                        with dve.Fori(0, T) as t:
                            here = dve.snap(t * SUB, min_val=0, max_val=(T - 1) * SUB)
                            dve.tensor_single_scalar(rel[:, :], dstf[:, ds(here, SUB)], basef[:, ds(t, 1)], ALU.subtract).then_inc(rel_set, 1)
                            windows = jobs.windows()
                            with dve.Fori(0, windows):
                                j = jobs.number()
                                node = jobs.first_node()
                                dve.wait_ge(rel_set, t + j + 1)
                                for h in range(2):
                                    dve.wait_ge(summed, SUB * j + HALF * (h + 1))
                                    dve.tensor_tensor(onehot[h][:, :, :], cols3.broadcast_to([P, HALF, WIN]),
                                                      rel[:, h * HALF:(h + 1) * HALF].rearrange("p (s o) -> p s o", o=1).broadcast_to([P, HALF, WIN]),
                                                      ALU.is_equal).then_inc(hot_set, 1)
                                for h in range(2):
                                    dve.wait_ge(hot_set, 2 * j + h + 1)
                                    dve.tensor_tensor(onehot[h][:, :, :], onehot[h][:, :, :],
                                                      wgt[:, ds(here + h * HALF, HALF)].rearrange("p (s o) -> p s o", o=1).broadcast_to([P, HALF, WIN]),
                                                      ALU.mult).then_inc(onehot_ready, 1)
                                jobs.read_ahead(t)
                                dve.wait_ge(onehot_ready, 2 * j + 2)
                                dve.tensor_single_scalar(rel[:, :], rel[:, :], float(WIN), ALU.subtract).then_inc(rel_set, 1)
                                dve.wait_ge(scat_set, j + 1)
                                for s in range(SUB):
                                    h, o = s // HALF, (s % HALF) * P
                                    if s % HALF == 0:
                                        dve.wait_ge(srcb_ready[h], 16 * (j + 1))
                                    ins = dve.scalar_tensor_tensor(eq[s][:, :], srcb[h][:, o:o + P], srcf[:, ds(here + s, 1)], tri[:, :],
                                                                   ALU.is_equal, ALU.mult, accum_out=dup[:, s:s + 1])
                                    if s % HALF == HALF - 1:
                                        ins.then_inc(dups_done, 1)
                                dve.wait_ge(x_loaded, 16)
                                dve.wait_ge(dups_done, done(j, 1))
                                dve.tensor_copy(repeats[:, ds(here, SUB)], dup[:, :]).then_inc(scat_set, 1)
                                for h in range(2):
                                    dve.wait_ge(summed, SUB * (j + 1) + HALF * (h + 1))
                                    dve.wait_ge(flushed, freed(j, h) + 1)
                                    dve.tensor_tensor(aggT[:, ds(node, WIN)], aggT[:, ds(node, WIN)], bank[h][:, 0:WIN],
                                                      ALU.add).then_inc(flushed, 1)
                                jobs.step()

            layer0_nodes(nc, sem, sb1, aggT, x_rows, x1_d, h1_parts, tabs[0], w_sb, b1c, bias3, ones3, ident, eps, zero, spare, bank,
                         wgt, dstf, srcf, repeats, spare_row, scat, scattered)
        layer0.close()
        with ExitStack() as c4:
            layer1_edges(nc, sem, lambda n, s, d: c4.enter_context(nc.sbuf_tensor(n, s, d)), src16, dst16, attr_cols,
                         h1_parts, tabs, srcf, wgt, scat, basef, base, nwin, pidx, spare_row,
                         ones3, zero, scattered, bias3, nn1, w_sb["nn2T"], bank)
        with ExitStack() as c5:
            layer1_nodes(nc, sem, lambda n, s, d: c5.enter_context(nc.sbuf_tensor(n, s, d)), x1_d, tabs, w_sb["lin2T"],
                         bias3, ones3, ident, eps, zero, spare, bank, out)


def done(c, h):
    return 2 * c + h + CREDIT + 1


def freed(c, h):
    return 2 * c + h + CREDIT - 1


class TileTable:

    def __init__(self, engine, name, nwin, base=None):
        self.engine, self.nwin, self.base = engine, nwin, base
        self.job, self.count, self.next_count, self.node, self.next_node = (
            engine.alloc_register(f"{name}_{r}") for r in ("job", "count", "next_count", "node", "next_node"))
        engine.reg_mov(self.job, 0)
        engine.reg_load(self.next_count, nwin[0:1, 0:1])
        if base is not None:
            engine.reg_load(self.next_node, base[0:1, 0:1])

    def windows(self):
        self.engine.reg_mov(self.count, self.next_count)
        if self.base is not None:
            self.engine.reg_mov(self.node, self.next_node)
        return self.engine.snap(self.count, min_val=1, max_val=-(-N // WIN))

    def number(self):
        return self.engine.snap(self.job, min_val=0, max_val=MAXJOBS)

    def first_node(self):
        return self.engine.snap(self.node, min_val=0, max_val=NPAD - WIN)

    def read_ahead(self, t):
        self.engine.reg_load(self.next_count, self.nwin[0:1, bass.ds(t + 1, 1)])
        if self.base is not None:
            self.engine.reg_load(self.next_node, self.base[0:1, bass.ds(t + 1, 1)])

    def step(self):
        self.engine.reg_add(self.job, self.job, 1)
        if self.base is not None:
            self.engine.reg_add(self.node, self.node, WIN)


def prime(engine, spare, semaphore, zero):
    engine.dma_start(spare, zero[0:1, 0:16]).then_inc(semaphore, 16)


def wait_apart(engine, semaphore, value, passed):
    engine.wait_ge(semaphore, value)
    engine.sem_inc(passed, 1)


LN_STEPS = 2 + 3 * G


def ln_step(c, h, k):
    return LN_STEPS * (2 * c + h + 2) + k


def rows_done(c, h):
    return G * (2 * c + h + 3)


def rows_freed(c, h):
    return G * (2 * c + h + 1)


Y_SET, VAR_SET, LN_DONE = 1, 1 + 2 * G, LN_STEPS


def layer_norm_stats(dve, steps, passed, c, h, y, stats, mean_var):
    wait_apart(dve, steps, ln_step(c, h, Y_SET), passed)
    for g in range(G):
        dve.bn_stats(stats[:, g, :], y[:, g, :]).then_inc(steps, 1)
    wait_apart(dve, steps, ln_step(c, h, 1 + G), passed)
    for g in range(G):
        dve.bn_aggr(mean_var[:, g, :], stats[:, g, :]).then_inc(steps, 1)


def layer_norm_rows(dve, steps, passed, c, h, y, mean_var, std, rstd, rows):
    dve.reciprocal(rstd[:, :], std[:, :]).then_inc(steps, 1)
    wait_apart(dve, steps, ln_step(c, h, VAR_SET + 1), passed)
    for g in range(G):
        dve.tensor_scalar(rows[:, g, :], y[:, g, :], mean_var[:, g, 0:1], rstd[:, g:g + 1],
                          mybir.AluOpType.subtract, mybir.AluOpType.mult).then_inc(steps, 1)


def layer_norm_factors(dve, steps, passed, c, h, mean_var, std, rstd, shift):
    dve.reciprocal(rstd[:, :], std[:, :]).then_inc(steps, 1)
    wait_apart(dve, steps, ln_step(c, h, VAR_SET + 1), passed)
    dve.scalar_tensor_tensor(shift[:, :], mean_var[:, :, 0], -1.0, rstd[:, :],
                             mybir.AluOpType.mult, mybir.AluOpType.mult).then_inc(steps, G)


def in_turn(engine, *stages, before_end=None):
    deepest = 3
    pairs = (UNITS - deepest) // 2
    for u in range(-deepest, 0):
        for ahead, stage in stages:
            if 0 <= u + ahead < UNITS:
                stage(0, u + ahead)
    if pairs > 0:
        with engine.Fori(0, pairs) as c:
            for h in range(2):
                for ahead, stage in stages:
                    stage(c, h + ahead)
    pairs = max(0, pairs)
    if before_end is not None:
        before_end()
    for u in range(2 * pairs, UNITS):
        for ahead, stage in stages:
            if u + ahead < UNITS:
                stage(pairs, u + ahead - 2 * pairs)


def unit_nodes(c, h):
    return bass.ds(c * 2 * UNIT + h * UNIT, UNIT)


def unit_rows(dram, c, h):
    return dram[unit_nodes(c, h), :].rearrange("(p g) d -> p g d", g=G)


def layer0_nodes(nc, sem, sbuf, aggT, x_rows, x1_d, h1_parts, tab0, w_sb, b1c, bias3, ones3, ident, eps, zero, spare, bank,
                 wgt, u, srcf, repeats, spare_row, scat, scattered):
    f32, bf16 = mybir.dt.float32, mybir.dt.bfloat16
    ALU, ACT = mybir.AluOpType, mybir.ActivationFunctionType
    two = lambda name, shape, dt=f32: [sbuf(f"n_{name}{k}", shape, dt) for k in range(2)]
    hidT, x1T = two("hidT", [P, G, P]), two("x1T", [P, UNIT])
    xr, y, x1, h1, rest = (two(n, [P, G, D]) for n in ("xr", "y", "x1", "h1", "rest"))
    parts = two("parts", [P, G, 3, D], bf16)
    stats, mean_var = two("stats", [P, G, 6]), two("mv", [P, G, 2])
    std, rstd = two("std", [P, G]), two("rstd", [P, G])
    up, down, turned, lin = (sem(f"n_{n}") for n in ("up", "down", "turned", "lin"))
    hid, std_set, x1T_set, h1_set, high_set, mid_set = (sem(f"n_{n}") for n in ("hid", "std", "x1T", "h1", "high", "mid"))
    rest_set, parts_set, steps, passed = (sem(f"n_{n}") for n in ("rest", "parts", "steps", "passed"))
    xr_in, x1_stored, h1_stored, parts_stored = ([sem(f"n_{n}{k}") for k in range(2)] for n in ("xr_in", "x1_st", "h1_st", "parts_st"))

    turns_buf = sbuf("turns", [P, T * SUB], f32)
    half_pi = sbuf("half_pi", [P, 1], f32)
    table_steps, sined = sem("c_steps"), sem("c_sined")
    magic = 1.5 * 2.0 ** 23

    def turns(c, h):
        return c + h // 2

    with nc.Block() as block:
        @block.sync
        def _(sp):
            def load(c, h):
                k = h % 2
                sp.wait_ge(steps, ln_step(c, h - 2, Y_SET))
                sp.dma_start(xr[k][:, :, :], unit_rows(x_rows, c, h)).then_inc(xr_in[k], 16)

            def store_x1(c, h):
                k = h % 2
                sp.wait_ge(steps, ln_step(c, h, LN_DONE))
                sp.dma_start(unit_rows(x1_d, c, h), x1[k][:, :, :]).then_inc(x1_stored[k], 16)

            def store_h1(c, h):
                k = h % 2
                sp.wait_ge(h1_set, done(c, h))
                sp.dma_start(unit_rows(tab0, c, h), h1[k][:, :, :]).then_inc(h1_stored[k], 16)

            def store_parts(c, h):
                k = h % 2
                sp.wait_ge(parts_set, done(c, h))
                sp.dma_start(unit_rows(h1_parts, c, h), parts[k][:, :, :, :].rearrange("p g k d -> p g (k d)")).then_inc(parts_stored[k], 16)

            for k in range(2):
                for i, stored in enumerate((x1_stored, h1_stored, parts_stored)):
                    prime(sp, spare[8 + 3 * k + i:9 + 3 * k + i, :], stored[k], zero)
            in_turn(sp, (3, load), (2, store_x1), (1, store_h1), (0, store_parts))
            for k in range(2):
                for stored in (x1_stored, h1_stored, parts_stored):
                    sp.wait_ge(stored[k], 16 * (1 + (UNITS + 1 - k) // 2))

        @block.tensor
        def _(pe):
            def first(c, h):
                k = h % 2
                pe.wait_ge(hid, freed(c, h))
                nc.tensor.matmul(bank[k][:, :], w_sb["W1"][:, :], aggT[:, unit_nodes(c, h)], start=True, stop=True).then_inc(up, 1)

            def second(c, h):
                k = h % 2
                pe.wait_ge(steps, ln_step(c, h - 2, Y_SET))
                nc.tensor.matmul(bank[2 + k][:, :], ones3[:, :], bias3["b2"][:, :], start=True, stop=False)
                pe.wait_ge(hid, done(c, h))
                for g in range(G):
                    ins = nc.tensor.matmul(bank[2 + k][:, g * P:g * P + P], hidT[k][:, g, :], w_sb["W2"][:, :],
                                           start=False, stop=(g == G - 1))
                ins.then_inc(down, 1)

            def turn(c, h):
                k = h % 2
                pe.wait_ge(steps, ln_step(c, h, LN_DONE))
                pe.wait_ge(x1T_set, freed(c, h))
                for g in range(G):
                    ins = nc.tensor.transpose(bank[4 + k][:, g * P:g * P + P], x1[k][:, g, :], ident[:, :])
                ins.then_inc(turned, 1)

            def linear(c, h):
                k = h % 2
                pe.wait_ge(x1T_set, done(c, h))
                pe.wait_ge(h1_set, freed(c, h))
                for g in range(G):
                    ins = nc.tensor.matmul(bank[6 + k][:, g * P:g * P + P], x1T[k][:, g * P:g * P + P], w_sb["lin1T"][:, :],
                                           start=True, stop=True)
                ins.then_inc(lin, 1)

            for s in (up, down, turned, lin):
                pe.sem_inc(s, CREDIT)
            in_turn(pe, (3, first), (2, second), (1, turn), (1, linear))

        @block.scalar
        def _(act):
            def relu(c, h):
                k = h % 2
                act.wait_ge(up, done(c, h))
                act.wait_ge(down, freed(c, h))
                nc.scalar.activation(hidT[k][:, :, :], bank[k][:, :].rearrange("f (p g) -> f g p", g=G), ACT.Relu,
                                     bias=b1c[:, 0:1]).then_inc(hid, 1)

            def root(c, h):
                k = h % 2
                act.wait_ge(steps, ln_step(c, h, VAR_SET))
                nc.scalar.activation(std[k][:, :], mean_var[k][:, :, 1], ACT.Sqrt, bias=eps[:, 0:1]).then_inc(std_set, 1)

            def take_x1T(c, h):
                k = h % 2
                act.wait_ge(turned, done(c, h))
                act.wait_ge(lin, freed(c, h))
                nc.scalar.activation(x1T[k][:, :], bank[4 + k][:, :], ACT.Copy).then_inc(x1T_set, 1)

            def take_h1(c, h):
                k = h % 2
                act.wait_ge(lin, done(c, h))
                act.wait_ge(h1_stored[k], 16 * (turns(c, h) + 1))
                act.wait_ge(rest_set, freed(c, h))
                nc.scalar.activation(h1[k][:, :, :], bank[6 + k][:, :].rearrange("p (g d) -> p g d", g=G),
                                     ACT.Copy).then_inc(h1_set, 1)
                act.wait_ge(parts_stored[k], 16 * (turns(c, h) + 1))
                act.wait_ge(h1_set, done(c, h))
                nc.scalar.activation(parts[k][:, :, 0, :], h1[k][:, :, :], ACT.Copy).then_inc(high_set, 1)
                act.wait_ge(rest_set, done(c, h))
                nc.scalar.activation(parts[k][:, :, 2, :], rest[k][:, :, :], ACT.Copy).then_inc(mid_set, 1)

            for s in (hid, std_set, x1T_set, h1_set, high_set, mid_set):
                act.sem_inc(s, CREDIT)
            def edge_tables():
                act.wait_ge(table_steps, 8)
                nc.scalar.activation(scat[:, :], turns_buf[:, :], ACT.Copy)
                nc.scalar.activation(u[:, :], u[:, :], ACT.Abs).then_inc(sined, 1)
                act.wait_ge(sined, 1)
                nc.scalar.activation(u[:, :], u[:, :], ACT.Sin, bias=half_pi[:, 0:1], scale=-PI / (2 * CUTOFF)).then_inc(sined, 1)

            in_turn(act, (3, relu), (1, take_x1T), (2, root), (1, take_h1), before_end=edge_tables)

        @block.gpsimd
        def _(pool):
            for k in range(2 * NTAB):
                if k >= NTAB:
                    pool.wait_ge(scattered[k % NTAB], 16)
                prime(pool, spare[16 + k:17 + k, :], scattered[k % NTAB], zero)
            v = turns_buf[:, :]
            pool.memset(half_pi[:, :], PI / 2).then_inc(table_steps, 1)
            pool.tensor_scalar(v, wgt[:, :], 1.0 / (2 * CUTOFF), magic, ALU.mult, ALU.add).then_inc(table_steps, 1)
            pool.wait_ge(table_steps, 2)
            pool.tensor_scalar(v, v, magic, -2 * CUTOFF, ALU.subtract, ALU.mult).then_inc(table_steps, 1)
            pool.wait_ge(table_steps, 3)
            pool.tensor_tensor(u[:, :], wgt[:, :], v, ALU.add).then_inc(table_steps, 1)
            pool.wait_ge(table_steps, 4)
            pool.tensor_single_scalar(repeats[:, :], repeats[:, :], 1.0, ALU.min).then_inc(table_steps, 1)
            pool.tensor_scalar(v, srcf[:, :], spare_row[:, 0:1], -1.0, ALU.subtract, ALU.mult).then_inc(table_steps, 1)
            pool.wait_ge(table_steps, 6)
            pool.tensor_tensor(v, v, repeats[:, :], ALU.mult).then_inc(table_steps, 1)
            pool.wait_ge(table_steps, 7)
            pool.tensor_tensor(v, v, srcf[:, :], ALU.add).then_inc(table_steps, 1)
            pool.wait_ge(sined, 2)
            pool.tensor_tensor(wgt[:, :], u[:, :], u[:, :], ALU.mult)
            for k in range(NTAB):
                pool.wait_ge(scattered[k], 32)

        @block.vector
        def _(dve):
            def residual(c, h):
                k = h % 2
                dve.wait_ge(down, done(c, h))
                dve.wait_ge(xr_in[k], 16 * (turns(c, h) + 1))
                dve.tensor_tensor(y[k][:, :, :], bank[2 + k][:, :].rearrange("p (g d) -> p g d", g=G),
                                  xr[k][:, :, :], ALU.add).then_inc(steps, 1)
                layer_norm_stats(dve, steps, passed, c, h, y[k], stats[k], mean_var[k])

            def norm(c, h):
                k = h % 2
                dve.wait_ge(std_set, done(c, h))
                dve.wait_ge(x1_stored[k], 16 * (turns(c, h) + 1))
                wait_apart(dve, turned, freed(c, h), passed)
                layer_norm_rows(dve, steps, passed, c, h, y[k], mean_var[k], std[k], rstd[k], x1[k])

            def second_part(c, h):
                k = h % 2
                dve.wait_ge(high_set, done(c, h))
                dve.wait_ge(parts_set, freed(c, h))
                dve.tensor_tensor(rest[k][:, :, :], h1[k][:, :, :], parts[k][:, :, 0, :], ALU.subtract).then_inc(rest_set, 1)

            def third_part(c, h):
                k = h % 2
                dve.wait_ge(mid_set, done(c, h))
                dve.wait_ge(rest_set, done(c, h))
                dve.tensor_tensor(parts[k][:, :, 1, :], rest[k][:, :, :], parts[k][:, :, 2, :], ALU.subtract).then_inc(parts_set, 1)

            for s in (rest_set, parts_set):
                dve.sem_inc(s, CREDIT)
            dve.sem_inc(steps, 2 * LN_STEPS)
            in_turn(dve, (2, residual), (0, third_part), (2, norm), (1, second_part))


def layer1_edges(nc, sem, sbuf, src16, dst16, attr_cols, h1_parts, tabs, srcf, wgt, scat, basef, base, nwin,
                 pidx, spare_row, ones3, zero, scattered, bias3, nn1, nn2T, bank):
    f32, i32, i16, bf16 = mybir.dt.float32, mybir.dt.int32, mybir.dt.int16, mybir.dt.bfloat16
    ALU, ACT, ds = mybir.AluOpType, mybir.ActivationFunctionType, bass.ds
    attr = [sbuf(f"attr{h}", [1 + GAUSS, HE], f32) for h in range(2)]
    dstb = [sbuf(f"dstb{h}", [P, HE], i16) for h in range(2)]
    srcb = [sbuf(f"srcb1{h}", [P, HE], i16) for h in range(2)]
    h1w = [sbuf(f"h1w{h}", [P, 2 * D], bf16) for h in range(2)]
    soft1 = [sbuf(f"soft1_{h}", [P, HE], f32) for h in range(2)]
    soft2 = [sbuf(f"soft2_{h}", [P, HE], f32) for h in range(2)]
    hid = [sbuf(f"hid{h}", [P, HE], f32) for h in range(2)]
    filt = [sbuf(f"filt{h}", [P, HE], f32) for h in range(2)]
    ohT = [sbuf(f"ohT{h}", [P, HE], bf16) for h in range(2)]
    same = [sbuf(f"same{s}", [P, P], f32) for s in range(SUB)]
    rows = [sbuf(f"rows{h}", [P, HE], f32) for h in range(2)]
    sidx_next = [sbuf(f"sidx_next{h}", [P, HALF], i32) for h in range(2)]
    sidx = [sbuf(f"sidx{h}", [P, HALF], i32) for h in range(2)]
    rel0 = sbuf("rel0", [P, 1], f32)

    attr_in, dstb_in, srcb_in, h1w_in = ([sem(f"{n}_in{h}") for h in range(2)] for n in ("attr", "dstb", "srcb", "h1w"))
    z1_set, z2_set, taken = sem("z1_set"), sem("z2_set"), sem("taken_set")
    abs1, exp1, ln1 = sem("abs1"), sem("exp1"), sem("ln1")
    abs2, exp2, ln2 = sem("abs2"), sem("exp2"), sem("ln2")
    oh_set, same_set, hid_set = sem("oh_set"), sem("same_set"), sem("hid_set")
    filt_set, msg_set = sem("filt_set"), sem("msg_set")
    merged = sem("merged")
    sidx_set, rows_set, stash_set = sem("sidx_set"), sem("rows_set"), sem("stash_set")
    rel_set, zeros_set, h1_finite = sem("rel1_set"), sem("zeros_set"), sem("h1_finite")
    passed, passed_sp = sem("e_passed_pool"), sem("e_passed_sp")

    with nc.Block() as block:
        @block.sync
        def _(sp):
            jobs = TileTable(sp, "sp1", nwin, base)
            with sp.Fori(0, T) as t:
                windows = jobs.windows()
                with sp.Fori(0, windows):
                    j = jobs.number()
                    node = jobs.first_node()
                    for h in range(2):
                        wait_apart(sp, z1_set, freed(j, h), passed_sp)
                        sp.dma_start(attr[h][:, :], attr_cols[:, ds(t * TE + h * HE, HE)]).then_inc(attr_in[h], 16)
                        wait_apart(sp, oh_set, freed(j, h), passed_sp)
                        sp.dma_start(dstb[h][:, :], dst16[ds(t, 1), h * HE:(h + 1) * HE].broadcast_to([P, HE])).then_inc(dstb_in[h], 16)
                        wait_apart(sp, same_set, freed(j, h), passed_sp)
                        sp.dma_start(srcb[h][:, :], src16[ds(t, 1), h * HE:(h + 1) * HE].broadcast_to([P, HE])).then_inc(srcb_in[h], 16)
                        wait_apart(sp, taken, freed(j, h), passed_sp)
                        sp.dma_start(h1w[h][0:WIN, :], h1_parts[ds(node, WIN), 0:2 * D]).then_inc(h1w_in[h], 16)
                        sp.dma_start(h1w[h][WIN:P, 0:D], h1_parts[ds(node, WIN), 2 * D:3 * D]).then_inc(h1w_in[h], 16)
                    jobs.read_ahead(t)
                    jobs.step()

        @block.tensor
        def _(pe):
            def first_layer(j, h):
                pe.wait_ge(attr_in[h], 16 * (j + 1))
                pe.wait_ge(hid_set, freed(j, h))
                nc.tensor.matmul(bank[h][:, :], nn1[:, :], attr[h][:, :], start=True, stop=True).then_inc(z1_set, 1)

            def take_h1(j, h):
                pe.wait_ge(oh_set, done(j, h))
                pe.wait_ge(h1w_in[h], 32 * (j + 1))
                pe.wait_ge(msg_set, freed(j, h))
                for s in range(HALF):
                    nc.tensor.matmul(bank[4 + h][:, s * P:s * P + P], ohT[h][:, s * P:s * P + P],
                                     h1w[h][:, 0:D], start=True, stop=False)
                    ins = nc.tensor.matmul(bank[4 + h][:, s * P:s * P + P], ohT[h][0:WIN, s * P:s * P + P],
                                           h1w[h][0:WIN, D:2 * D], start=False, stop=True)
                ins.then_inc(taken, 1)

            def second_layer(j, h):
                pe.wait_ge(filt_set, freed(j, h))
                nc.tensor.matmul(bank[2 + h][:, :], ones3[:, :], bias3["nnb2"][:, :], start=True, stop=False)
                pe.wait_ge(hid_set, done(j, h))
                for s in range(HALF):
                    ins = nc.tensor.matmul(bank[2 + h][:, s * P:s * P + P], hid[h][:, s * P:s * P + P], nn2T[:, :],
                                           start=False, stop=(s == HALF - 1))
                ins.then_inc(z2_set, 1)

            def merge_before(j, h):
                pe.wait_ge(msg_set, freed(j, h))
                pe.wait_ge(rows_set, freed(j - 1, h))
                for s in range(HALF):
                    ins = nc.tensor.matmul(bank[6 + h][:, s * P:s * P + P], same[h * HALF + s][:, :],
                                           filt[h][:, s * P:s * P + P], start=True, stop=True)
                ins.then_inc(merged, 1)

            for s in (z1_set, taken):
                pe.sem_inc(s, CREDIT)
            pe.sem_inc(z2_set, CREDIT - 1)
            pe.sem_inc(merged, CREDIT - 2)
            pe.wait_ge(zeros_set, SUB + 2)
            nc.tensor.matmul(bank[5][:, :], ones3[:, :], bias3["nnb2"][:, :], start=True, stop=True).then_inc(h1_finite, 1)
            jobs = TileTable(pe, "pe1", nwin)
            with pe.Fori(0, T) as t:
                windows = jobs.windows()
                with pe.Fori(0, windows):
                    j = jobs.number()
                    first_layer(j, 0)
                    second_layer(j - 1, 1)
                    merge_before(j, 0)
                    first_layer(j, 1)
                    second_layer(j, 0)
                    jobs.read_ahead(t)
                    take_h1(j, 0)
                    merge_before(j, 1)
                    take_h1(j, 1)
                    jobs.step()
            end = jobs.number()
            second_layer(end - 1, 1)
            merge_before(end, 0)
            merge_before(end, 1)

        @block.scalar
        def _(act):
            def absolute(j, h, z, buf, made, used, s_abs):
                act.wait_ge(made, done(j, h))
                act.wait_ge(used, freed(j, h))
                nc.scalar.activation(buf[:, :], z[:, :], ACT.Abs).then_inc(s_abs, 1)

            def exponential(j, h, buf, s_abs, s_exp):
                act.wait_ge(s_abs, done(j, h))
                nc.scalar.activation(buf[:, :], buf[:, :], ACT.Exp, scale=-1.0).then_inc(s_exp, 1)

            def logarithm(j, h, buf, s_exp, s_ln):
                act.wait_ge(s_exp, done(j, h))
                nc.scalar.activation(buf[:, :], buf[:, :], ACT.Ln, bias=0.5, scale=0.5).then_inc(s_ln, 1)

            def abs_1(j, h):
                absolute(j, h, bank[h], soft1[h], z1_set, hid_set, abs1)

            def exp_1(j, h):
                exponential(j, h, soft1[h], abs1, exp1)

            def ln_1(j, h):
                logarithm(j, h, soft1[h], exp1, ln1)

            def abs_2(j, h):
                absolute(j, h, bank[2 + h], soft2[h], z2_set, filt_set, abs2)

            def exp_2(j, h):
                exponential(j, h, soft2[h], abs2, exp2)

            def ln_2(j, h):
                logarithm(j, h, soft2[h], exp2, ln2)

            def places_before(j, h):
                for s in range(HALF):
                    act.wait_ge(scattered[s], 16 * (2 * j + h + 1))
                act.wait_ge(stash_set, freed(j, h))
                nc.scalar.activation(sidx[h][:, :], sidx_next[h][:, :], ACT.Copy).then_inc(sidx_set, 1)

            def rows_before(j, h):
                act.wait_ge(merged, freed(j, h))
                nc.scalar.activation(rows[h][:, :], bank[6 + h][:, :], ACT.Copy).then_inc(rows_set, 1)

            def stash_rows(j, h, here):
                act.wait_ge(sidx_set, freed(j, h))
                nc.scalar.activation(sidx_next[h][:, :], scat[:, ds(here + h * HALF, HALF)], ACT.Copy).then_inc(stash_set, 1)

            nc.scalar.preload_act_table_set("natural_log_exp_and_others")
            for s in (abs1, exp1, ln1):
                act.sem_inc(s, CREDIT)
            for s in (abs2, exp2, ln2):
                act.sem_inc(s, CREDIT - 1)
            for s in (rows_set, sidx_set, stash_set):
                act.sem_inc(s, CREDIT - 2)
            for h in range(2):
                nc.scalar.activation(sidx_next[h][:, :], spare_row[:, 0:1].broadcast_to([P, HALF]), ACT.Copy).then_inc(stash_set, 1)
            act.wait_ge(h1_finite, 1)
            jobs = TileTable(act, "act1", nwin)
            with act.Fori(0, T) as t:
                windows = jobs.windows()
                here = act.snap(t * SUB, min_val=0, max_val=(T - 1) * SUB)
                with act.Fori(0, windows):
                    j = jobs.number()
                    abs_1(j, 0)
                    exp_1(j, 0)
                    abs_2(j - 1, 1)
                    ln_1(j, 0)
                    places_before(j, 0)
                    exp_2(j - 1, 1)
                    rows_before(j, 0)
                    ln_2(j - 1, 1)
                    abs_1(j, 1)
                    stash_rows(j, 0, here)
                    jobs.read_ahead(t)
                    exp_1(j, 1)
                    abs_2(j, 0)
                    ln_1(j, 1)
                    exp_2(j, 0)
                    places_before(j, 1)
                    ln_2(j, 0)
                    rows_before(j, 1)
                    stash_rows(j, 1, here)
                    jobs.step()
            end = jobs.number()
            abs_2(end - 1, 1)
            exp_2(end - 1, 1)
            ln_2(end - 1, 1)
            for h in range(2):
                places_before(end, h)
                rows_before(end, h)

        @block.gpsimd
        def _(pool):
            def scatter_before(j, h):
                pool.wait_ge(sidx_set, freed(j, h))
                for s in range(HALF):
                    pool.wait_ge(scattered[s], 16 * (2 * j + h + 2))
                    if s == 0:
                        wait_apart(pool, rows_set, freed(j, h), passed)
                    else:
                        pool.sem_inc(passed, 1)
                    pool.indirect_dma_start(tabs[s], bass.IndirectOffsetOnAxis(ap=sidx[h][:, s:s + 1], axis=0),
                                            rows[h][:, s * P:s * P + P], None, compute_op=ALU.add).then_inc(scattered[s], 16)

            jobs = TileTable(pool, "pool1", nwin)
            with pool.Fori(0, T) as t:
                windows = jobs.windows()
                with pool.Fori(0, windows):
                    j = jobs.number()
                    scatter_before(j, 0)
                    jobs.read_ahead(t)
                    scatter_before(j, 1)
                    jobs.step()
            end = jobs.number()
            scatter_before(end, 0)
            scatter_before(end, 1)
            for s in range(NTAB):
                pool.wait_ge(scattered[s], 16 * (2 * end + 4))

        @block.vector
        def _(dve):
            def one_hot(j, h):
                dve.wait_ge(dstb_in[h], 16 * (j + 1))
                dve.wait_ge(taken, freed(j, h))
                dve.tensor_single_scalar(ohT[h][:, :], dstb[h][:, :], rel0[:, 0:1], ALU.is_equal).then_inc(oh_set, 1)

            def equal_src(j, h, here):
                dve.wait_ge(srcb_in[h], 16 * (j + 1))
                dve.wait_ge(merged, freed(j, h))
                for s in range(HALF):
                    at = ds(here + h * HALF + s, 1)
                    ins = dve.tensor_scalar(same[h * HALF + s][:, :], srcb[h][:, s * P:s * P + P], srcf[:, at], wgt[:, at],
                                            ALU.is_equal, ALU.mult)
                ins.then_inc(same_set, 1)

            def hidden(j, h):
                dve.wait_ge(ln1, done(j, h))
                dve.wait_ge(z2_set, freed(j, h))
                dve.scalar_tensor_tensor(hid[h][:, :], bank[h][:, :], 0.0, soft1[h][:, :], ALU.max, ALU.add).then_inc(hid_set, 1)

            def message(j, h, merges):
                dve.wait_ge(ln2, done(j, h))
                dve.wait_ge(merged, merges)
                dve.scalar_tensor_tensor(filt[h][:, :], bank[2 + h][:, :], 0.0, soft2[h][:, :], ALU.max, ALU.add).then_inc(filt_set, 1)
                dve.wait_ge(taken, done(j, h))
                dve.wait_ge(filt_set, done(j, h))
                dve.tensor_tensor(filt[h][:, :], filt[h][:, :], bank[4 + h][:, :], ALU.mult).then_inc(msg_set, 1)

            for s in (oh_set, same_set, hid_set):
                dve.sem_inc(s, CREDIT)
            for s in (filt_set, msg_set):
                dve.sem_inc(s, CREDIT - 1)
            dve.sem_inc(rel_set, 1)
            dve.memset(hid[1][:, :], 0.0).then_inc(zeros_set, 1)
            dve.memset(filt[0][:, :], 0.0).then_inc(zeros_set, 1)
            for s in range(SUB):
                dve.memset(same[s][:, :], 0.0).then_inc(zeros_set, 1)
            jobs = TileTable(dve, "dve1", nwin)
            with dve.Fori(0, T) as t:
                windows = jobs.windows()
                j0 = jobs.number()
                here = dve.snap(t * SUB, min_val=0, max_val=(T - 1) * SUB)
                dve.wait_ge(rel_set, t + j0 + 1)
                dve.tensor_tensor(rel0[:, :], pidx[:, :], basef[:, ds(t, 1)], ALU.add).then_inc(rel_set, 1)
                with dve.Fori(0, windows):
                    j = jobs.number()
                    dve.wait_ge(rel_set, t + j + 2)
                    one_hot(j, 0)
                    hidden(j, 0)
                    equal_src(j, 0, here)
                    message(j - 1, 1, freed(j - 1, 1))
                    one_hot(j, 1)
                    hidden(j, 1)
                    jobs.read_ahead(t)
                    equal_src(j, 1, here)
                    message(j, 0, freed(j, 0))
                    dve.wait_ge(oh_set, done(j, 1))
                    dve.tensor_single_scalar(rel0[:, :], rel0[:, :], float(WIN), ALU.add).then_inc(rel_set, 1)
                    jobs.step()
            message(jobs.number() - 1, 1, freed(jobs.number() - 1, 1))


def layer1_nodes(nc, sem, sbuf, x1_d, tabs, lin2T, bias3, ones3, ident, eps, zero, spare, bank, out):
    f32 = mybir.dt.float32
    ALU, ACT = mybir.AluOpType, mybir.ActivationFunctionType
    two = lambda name, shape: [sbuf(f"f_{name}{k}", shape, f32) for k in range(2)]
    tab = two("tab", [P, NTAB, G, D])
    h2T = two("h2T", [P, UNIT])
    x1, y, o = (two(n, [P, G, D]) for n in ("x1", "y", "o"))
    stats, mean_var = two("stats", [P, G, 6]), two("mv", [P, G, 2])
    std, rstd, shift = two("std", [P, G]), two("rstd", [P, G]), two("shift", [P, G])
    turned, lin = sem("f_turned"), sem("f_lin")
    h2T_set, std_set = sem("f_h2T"), sem("f_std")
    o_set, passed_act = sem("f_o"), sem("f_passed_act")
    paired, summed, steps, passed = (sem(f"f_{n}") for n in ("paired", "summed", "steps", "passed"))
    tab_in, x1_in, stored = ([sem(f"f_{n}{k}") for k in range(2)] for n in ("tab_in", "x1_in", "stored"))

    with nc.Block() as block:
        @block.sync
        def _(sp):
            def load_tables(c, h):
                k = h % 2
                for i, read in ((2, paired), (3, paired), (1, summed), (0, turned)):
                    sp.wait_ge(read, freed(c, h))
                    sp.dma_start(tab[k][:, i, :, :], unit_rows(tabs[i], c, h)).then_inc(tab_in[k], 16)

            def load_x1(c, h):
                k = h % 2
                sp.wait_ge(steps, ln_step(c, h - 2, Y_SET))
                sp.dma_start(x1[k][:, :, :], unit_rows(x1_d, c, h)).then_inc(x1_in[k], 16)

            in_turn(sp, (2, load_tables), (1, load_x1))

        @block.tensor
        def _(pe):
            def turn(c, h):
                k = h % 2
                pe.wait_ge(summed, done(c, h))
                pe.wait_ge(h2T_set, freed(c, h))
                for g in range(G):
                    ins = nc.tensor.transpose(bank[k][:, g * P:g * P + P], tab[k][:, 0, g, :], ident[:, :])
                ins.then_inc(turned, 1)

            def linear(c, h):
                k = h % 2
                pe.wait_ge(steps, ln_step(c, h - 2, Y_SET))
                nc.tensor.matmul(bank[2 + k][:, :], ones3[:, :], bias3["lin2b"][:, :], start=True, stop=False)
                pe.wait_ge(h2T_set, done(c, h))
                for g in range(G):
                    ins = nc.tensor.matmul(bank[2 + k][:, g * P:g * P + P], h2T[k][:, g * P:g * P + P], lin2T[:, :],
                                           start=False, stop=(g == G - 1))
                ins.then_inc(lin, 1)

            for s in (turned, lin):
                pe.sem_inc(s, CREDIT)
            in_turn(pe, (1, linear), (2, turn))

        @block.scalar
        def _(act):
            def take_h2T(c, h):
                k = h % 2
                act.wait_ge(turned, done(c, h))
                act.wait_ge(lin, freed(c, h))
                nc.scalar.activation(h2T[k][:, :], bank[k][:, :], ACT.Copy).then_inc(h2T_set, 1)

            def root(c, h):
                k = h % 2
                act.wait_ge(steps, ln_step(c, h, VAR_SET))
                nc.scalar.activation(std[k][:, :], mean_var[k][:, :, 1], ACT.Sqrt, bias=eps[:, 0:1]).then_inc(std_set, 1)

            def norm(c, h):
                k = h % 2
                act.wait_ge(steps, ln_step(c, h, LN_DONE))
                wait_apart(act, stored[k], 16 * (c + h // 2 + 1), passed_act)
                for g in range(G):
                    nc.scalar.activation(o[k][:, g, :], y[k][:, g, :], ACT.Identity,
                                         bias=shift[k][:, g:g + 1], scale=rstd[k][:, g:g + 1]).then_inc(o_set, 1)

            for s in (h2T_set, std_set):
                act.sem_inc(s, CREDIT)
            act.sem_inc(o_set, 2 * G)
            in_turn(act, (0, root), (2, take_h2T), (0, norm))

        @block.gpsimd
        def _(pool):
            def store(c, h):
                k = h % 2
                pool.wait_ge(o_set, rows_done(c, h))
                pool.dma_start(unit_rows(out, c, h), o[k][:, :, :]).then_inc(stored[k], 16)

            for k in range(2):
                prime(pool, spare[24 + k:25 + k, :], stored[k], zero)
            in_turn(pool, (0, store))
            for k in range(2):
                pool.wait_ge(stored[k], 16 * (1 + (UNITS + 1 - k) // 2))

        @block.vector
        def _(dve):
            def add_tables(c, h):
                k = h % 2
                dve.wait_ge(tab_in[k], 16 * NTAB * (c + h // 2 + 1))
                dve.tensor_tensor(tab[k][:, 0:2, :, :], tab[k][:, 0:2, :, :], tab[k][:, 2:4, :, :], ALU.add).then_inc(paired, 1)
                dve.wait_ge(paired, done(c, h))
                dve.tensor_tensor(tab[k][:, 0, :, :], tab[k][:, 0, :, :], tab[k][:, 1, :, :], ALU.add).then_inc(summed, 1)

            def residual(c, h):
                k = h % 2
                dve.wait_ge(o_set, rows_freed(c, h))
                dve.wait_ge(lin, done(c, h))
                dve.wait_ge(x1_in[k], 16 * (c + h // 2 + 1))
                dve.tensor_tensor(y[k][:, :, :], bank[2 + k][:, :].rearrange("p (g d) -> p g d", g=G),
                                  x1[k][:, :, :], ALU.add).then_inc(steps, 1)
                layer_norm_stats(dve, steps, passed, c, h, y[k], stats[k], mean_var[k])

            def factors(c, h):
                k = h % 2
                dve.wait_ge(std_set, done(c, h))
                wait_apart(dve, o_set, rows_freed(c, h), passed)
                layer_norm_factors(dve, steps, passed, c, h, mean_var[k], std[k], rstd[k], shift[k])

            for s in (paired, summed):
                dve.sem_inc(s, CREDIT)
            dve.sem_inc(steps, 2 * LN_STEPS)
            in_turn(dve, (0, residual), (2, add_tables), (0, factors))


_OUTS = [((NPAD, D), "float32")]


def kernel(x, src, dst, edge_attr_50, edge_weight, L0_gnn_W1, L0_gnn_b1, L0_gnn_W2, L0_gnn_b2,
           L1_gnn_lin1_w, L1_gnn_nn_w1, L1_gnn_nn_b1, L1_gnn_nn_w2, L1_gnn_nn_b2, L1_gnn_lin2_w, L1_gnn_lin2_b):
    import numpy as np
    import concourse.bacc as bacc
    from concourse.bass_utils import run_bass_kernel_spmd

    x, src, dst, attr, w = (np.asarray(a) for a in (x, src, dst, edge_attr_50, edge_weight))
    pad = EPAD - E
    src = np.concatenate([src, np.arange(N, N + pad, dtype=src.dtype)])
    dst = np.concatenate([dst, np.full(pad, N - 1, dst.dtype)])
    w = np.concatenate([w, np.zeros(pad, w.dtype)])
    xp = np.zeros((NPAD, D), x.dtype)
    xp[:N] = x
    at = np.zeros((1 + GAUSS, EPAD), attr.dtype)
    at[0] = 1
    at[1:, :E] = attr.T

    def cols(a):
        return np.ascontiguousarray(a.reshape(T * SUB, P).T)

    row = lambda a: np.asarray(a).reshape(1, D)
    tr = lambda a: np.ascontiguousarray(np.asarray(a).T)
    ins = {
        "x_rows": xp, "x_cols": tr(xp), "src_cols": cols(src), "dst_cols": cols(dst), "w_cols": cols(w),
        "src_rows": src.reshape(T, TE), "dst_rows": dst.reshape(T, TE), "attr_cols": at,
        "W1": np.asarray(L0_gnn_W1), "b1": np.asarray(L0_gnn_b1).reshape(D, 1), "W2": np.asarray(L0_gnn_W2),
        "b2": row(L0_gnn_b2), "lin1T": tr(L1_gnn_lin1_w),
        "nn1T": np.concatenate([row(L1_gnn_nn_b1), tr(L1_gnn_nn_w1)]), "nn2T": tr(L1_gnn_nn_w2),
        "nnb2": row(L1_gnn_nn_b2), "lin2T": tr(L1_gnn_lin2_w), "lin2b": row(L1_gnn_lin2_b),
    }
    nc = bacc.Bacc("TRN2", target_bir_lowering=False, num_devices=1)
    args = {n: nc.dram_tensor(n, a.shape, mybir.dt.from_np(a.dtype), kind="ExternalInput").ap() for n, a in ins.items()}
    out = nc.dram_tensor("out", (NPAD, D), mybir.dt.float32, kind="ExternalOutput").ap()
    edge_network_kernel(nc, out=out, **args)
    r = run_bass_kernel_spmd(nc, [ins], core_ids=[0])
    return r.results[0]["out"][:N]
```
